# Optimizing a Trainium2 kernel written in Bass

```python
import numpy as np
import jax
import jax.numpy as jnp

def _softmax(x, axis=-1):
    return jax.nn.softmax(x, axis=axis)

def _gelu(x):
    return jax.nn.gelu(x, approximate=True)

def _silu(x):
    return jax.nn.silu(x)

def _sigmoid(x):
    return jax.nn.sigmoid(x)

def _layernorm(x, axis=-1, eps=1e-05):
    m = jnp.mean(x, axis=axis, keepdims=True)
    v = jnp.var(x, axis=axis, keepdims=True)
    return (x - m) / jnp.sqrt(v + eps)

def _scatter_add(tgt, idx, src, axis=0):
    return tgt.at[idx].add(src)

def _segment_sum(src, seg, n):
    return jax.ops.segment_sum(src, seg, n)
kernel_name = 'mk_prb_d1_jaxref_r8_c2b5ee'

def setup_inputs(seed: int=0):
    np.random.seed(seed)
    _w = jnp.asarray

    def _L0_attn_setup():
        import jax, jax.numpy as jnp
        import numpy as np
        D_MODEL = 128
        NUM_HEADS = 16
        DEPTH = D_MODEL // NUM_HEADS
        EPS_LN = 0.001
        EPS_QK = 1e-06

        def _split_heads(t):
            B, L, _ = t.shape
            return t.reshape(B, L, NUM_HEADS, DEPTH).transpose(0, 2, 1, 3)

        def _forward(x, Wq, bq, Wk, bk, Wv, bv, Wq2, bq2, Wk2, bk2, Wv2, bv2, Wo, bo, gamma, beta):
            B, L, _ = x.shape
            q = x @ Wq + bq
            k = x @ Wk + bk
            v = x @ Wv + bv
            q = _split_heads(q @ Wq2 + bq2)
            k = _split_heads(k @ Wk2 + bk2)
            v = _split_heads(v @ Wv2 + bv2)
            q = jax.nn.elu(q) + 1.0
            k = jax.nn.elu(k) + 1.0
            S = jnp.einsum('bhld,bhle->bhde', k, q)
            out = jnp.einsum('bhmd,bhde->bhme', v, S)
            qks = jnp.einsum('bhld,bhld->bhl', q, k) + EPS_QK
            out = out / qks[..., None]
            out = out.transpose(0, 2, 1, 3).reshape(B, L, D_MODEL)
            out = out @ Wo + bo
            y = x + out
            mu = jnp.mean(y, axis=-1, keepdims=True)
            var = jnp.var(y, axis=-1, keepdims=True)
            return gamma * (y - mu) * jax.lax.rsqrt(var + EPS_LN) + beta
        key = jax.random.key(seed)
        ks = jax.random.split(key, 16)
        s = 1.0 / np.sqrt(D_MODEL)

        def W(k):
            return jax.random.normal(k, (D_MODEL, D_MODEL), jnp.float32) * s

        def b(k):
            return jnp.zeros((D_MODEL,), jnp.float32)
        return {'x': jax.random.normal(ks[0], (4, 512, D_MODEL), jnp.float32), 'Wq': W(ks[1]), 'bq': b(ks[1]), 'Wk': W(ks[2]), 'bk': b(ks[2]), 'Wv': W(ks[3]), 'bv': b(ks[3]), 'Wq2': W(ks[4]), 'bq2': b(ks[4]), 'Wk2': W(ks[5]), 'bk2': b(ks[5]), 'Wv2': W(ks[6]), 'bv2': b(ks[6]), 'Wo': W(ks[7]), 'bo': b(ks[7]), 'gamma': jnp.ones((D_MODEL,), jnp.float32), 'beta': jnp.zeros((D_MODEL,), jnp.float32)}
    _L0_attn_in = _L0_attn_setup()

    def _L0_ffn_setup():
        import jax, jax.numpy as jnp
        import numpy as np
        TOPK = 8
        NUM_EXPERTS = 64
        FFN = 384
        CAPACITY = 160

        def _swiglu(x, w1, w2):
            h = x @ w1.T
            x1, x2 = jnp.split(h, 2, axis=-1)
            return x1 * jax.nn.silu(x2) @ w2.T
        key = jax.random.key(seed)
        ks = jax.random.split(key, 6)
        B, S, H = (1, 64, 128)
        scale = 0.02
        return {'hidden_states': jax.random.normal(ks[0], (B, S, H), jnp.float32), 'wg': jax.random.normal(ks[1], (NUM_EXPERTS, H), jnp.float32) * scale, 'shared_w1': jax.random.normal(ks[2], (2 * FFN, H), jnp.float32) * scale, 'shared_w2': jax.random.normal(ks[3], (H, FFN), jnp.float32) * scale, 'expert_w1': jax.random.normal(ks[4], (NUM_EXPERTS, 2 * FFN, H), jnp.float32) * scale, 'expert_w2': jax.random.normal(ks[5], (NUM_EXPERTS, H, FFN), jnp.float32) * scale}
    _L0_ffn_in = _L0_ffn_setup()
    _d = {'L0_attn_x': _L0_attn_in['x'], 'L0_attn_Wq': _L0_attn_in['Wq'], 'L0_attn_bq': _L0_attn_in['bq'], 'L0_attn_Wk': _L0_attn_in['Wk'], 'L0_attn_bk': _L0_attn_in['bk'], 'L0_attn_Wv': _L0_attn_in['Wv'], 'L0_attn_bv': _L0_attn_in['bv'], 'L0_attn_Wq2': _L0_attn_in['Wq2'], 'L0_attn_bq2': _L0_attn_in['bq2'], 'L0_attn_Wk2': _L0_attn_in['Wk2'], 'L0_attn_bk2': _L0_attn_in['bk2'], 'L0_attn_Wv2': _L0_attn_in['Wv2'], 'L0_attn_bv2': _L0_attn_in['bv2'], 'L0_attn_Wo': _L0_attn_in['Wo'], 'L0_attn_bo': _L0_attn_in['bo'], 'L0_attn_gamma': _L0_attn_in['gamma'], 'L0_attn_beta': _L0_attn_in['beta'], 'L0_ffn_wg': _L0_ffn_in['wg'], 'L0_ffn_shared_w1': _L0_ffn_in['shared_w1'], 'L0_ffn_shared_w2': _L0_ffn_in['shared_w2'], 'L0_ffn_expert_w1': _L0_ffn_in['expert_w1'], 'L0_ffn_expert_w2': _L0_ffn_in['expert_w2']}
    _x0 = _d['L0_attn_x']
    _d['L0_attn_x'] = jax.random.normal(jax.random.fold_in(jax.random.key(seed), 1), (16, 256, 128), dtype=_x0.dtype)
    del _x0
    return _d

def reference(L0_attn_x, L0_attn_Wq, L0_attn_bq, L0_attn_Wk, L0_attn_bk, L0_attn_Wv, L0_attn_bv, L0_attn_Wq2, L0_attn_bq2, L0_attn_Wk2, L0_attn_bk2, L0_attn_Wv2, L0_attn_bv2, L0_attn_Wo, L0_attn_bo, L0_attn_gamma, L0_attn_beta, L0_ffn_wg, L0_ffn_shared_w1, L0_ffn_shared_w2, L0_ffn_expert_w1, L0_ffn_expert_w2):

    def _L0_attn_ref(x, Wq, bq, Wk, bk, Wv, bv, Wq2, bq2, Wk2, bk2, Wv2, bv2, Wo, bo, gamma, beta):
        import jax, jax.numpy as jnp
        import numpy as np
        D_MODEL = 128
        NUM_HEADS = 16
        DEPTH = D_MODEL // NUM_HEADS
        EPS_LN = 0.001
        EPS_QK = 1e-06

        def _split_heads(t):
            B, L, _ = t.shape
            return t.reshape(B, L, NUM_HEADS, DEPTH).transpose(0, 2, 1, 3)

        def _forward(x, Wq, bq, Wk, bk, Wv, bv, Wq2, bq2, Wk2, bk2, Wv2, bv2, Wo, bo, gamma, beta):
            B, L, _ = x.shape
            q = x @ Wq + bq
            k = x @ Wk + bk
            v = x @ Wv + bv
            q = _split_heads(q @ Wq2 + bq2)
            k = _split_heads(k @ Wk2 + bk2)
            v = _split_heads(v @ Wv2 + bv2)
            q = jax.nn.elu(q) + 1.0
            k = jax.nn.elu(k) + 1.0
            S = jnp.einsum('bhld,bhle->bhde', k, q)
            out = jnp.einsum('bhmd,bhde->bhme', v, S)
            qks = jnp.einsum('bhld,bhld->bhl', q, k) + EPS_QK
            out = out / qks[..., None]
            out = out.transpose(0, 2, 1, 3).reshape(B, L, D_MODEL)
            out = out @ Wo + bo
            y = x + out
            mu = jnp.mean(y, axis=-1, keepdims=True)
            var = jnp.var(y, axis=-1, keepdims=True)
            return gamma * (y - mu) * jax.lax.rsqrt(var + EPS_LN) + beta
        return _forward(x, Wq, bq, Wk, bk, Wv, bv, Wq2, bq2, Wk2, bk2, Wv2, bv2, Wo, bo, gamma, beta)

    def _L0_ffn_ref(hidden_states, wg, shared_w1, shared_w2, expert_w1, expert_w2):
        import jax, jax.numpy as jnp
        import numpy as np
        TOPK = 8
        NUM_EXPERTS = 64
        FFN = 384
        CAPACITY = 160

        def _swiglu(x, w1, w2):
            h = x @ w1.T
            x1, x2 = jnp.split(h, 2, axis=-1)
            return x1 * jax.nn.silu(x2) @ w2.T
        B, S, H = hidden_states.shape
        T = B * S
        x = hidden_states.reshape(T, H)
        shared_out = _swiglu(x, shared_w1, shared_w2)
        logits = x.astype(jnp.float32) @ wg.T
        gates = jax.nn.softmax(logits, axis=-1)
        w_topk, idx_topk = jax.lax.top_k(gates, TOPK)
        denom = jnp.maximum(w_topk.sum(-1, keepdims=True), jnp.finfo(jnp.float32).eps)
        w_topk = w_topk / denom
        A = T * TOPK
        flat_e = idx_topk.reshape(A)
        flat_w = w_topk.reshape(A)
        flat_t = jnp.repeat(jnp.arange(T), TOPK)
        order = jnp.argsort(flat_e)
        se, st, sw = (flat_e[order], flat_t[order], flat_w[order])
        counts = jnp.zeros(NUM_EXPERTS, jnp.int32).at[flat_e].add(1)
        starts = jnp.cumsum(counts) - counts
        rank = jnp.arange(A) - starts[se]
        valid = rank < CAPACITY
        buf = jnp.zeros((NUM_EXPERTS, CAPACITY, H), x.dtype).at[se, rank].set(x[st], mode='drop')
        h = jnp.einsum('ech,efh->ecf', buf, expert_w1)
        x1, x2 = jnp.split(h, 2, axis=-1)
        out = jnp.einsum('ecf,ehf->ech', x1 * jax.nn.silu(x2), expert_w2)
        y = out[se, jnp.clip(rank, 0, CAPACITY - 1)]
        y = jnp.where(valid[:, None], y * sw[:, None].astype(y.dtype), 0.0)
        combined = jnp.zeros((T, H), x.dtype).at[st].add(y)
        return (shared_out + combined).reshape(B, S, H)
    x = L0_attn_x
    xn = _layernorm(x, axis=-1)
    x = x + _L0_attn_ref(xn, L0_attn_Wq, L0_attn_bq, L0_attn_Wk, L0_attn_bk, L0_attn_Wv, L0_attn_bv, L0_attn_Wq2, L0_attn_bq2, L0_attn_Wk2, L0_attn_bk2, L0_attn_Wv2, L0_attn_bv2, L0_attn_Wo, L0_attn_bo, L0_attn_gamma, L0_attn_beta) + _L0_ffn_ref(xn, L0_ffn_wg, L0_ffn_shared_w1, L0_ffn_shared_w2, L0_ffn_expert_w1, L0_ffn_expert_w2)
    return x

_drawn_inputs = setup_inputs


def setup_inputs(seed=0):
    import zlib

    import numpy as np

    out = dict(_drawn_inputs(seed))
    spreads = {'L0_attn_bq': (0.0, 0.8),
     'L0_attn_bk': (0.0, 0.752),
     'L0_attn_bv': (0.0, 0.57),
     'L0_attn_bq2': (0.0, 0.8),
     'L0_attn_bk2': (0.0, 0.8),
     'L0_attn_bv2': (0.0, 0.421),
     'L0_attn_bo': (0.0, 2.0),
     'L0_attn_gamma': (1.0, 0.2),
     'L0_attn_beta': (0.0, 0.655)}
    factors = {'L0_ffn_wg': 8.0,
     'L0_ffn_shared_w1': 8.0,
     'L0_ffn_shared_w2': 8.0,
     'L0_ffn_expert_w1': 8.0,
     'L0_ffn_expert_w2': 8.0}
    for name, (base, spread) in spreads.items():
        noise = np.random.default_rng([zlib.crc32(name.encode()), seed]).standard_normal(out[name].shape)
        drawn = base * np.exp(spread * noise) if base else spread * noise
        out[name] = jnp.asarray(drawn.astype(out[name].dtype))
    for name, factor in factors.items():
        out[name] = (out[name] * factor).astype(out[name].dtype)
    return out
```

```python
import concourse.bass as bass
from concourse import mybir
from contextlib import ExitStack



def moments(eng, s, t, mean, var, step, k, eps, done):
    ALU = mybir.AluOpType
    t0, t1, t2 = t[:, 0, :], t[:, 1, :], t[:, 2, :]
    eng.tensor_tensor(t0, s[:, :, 1], s[:, :, 4], ALU.add).then_inc(step, 1)
    eng.tensor_tensor(t1, s[:, :, 1], s[:, :, 4], ALU.subtract).then_inc(step, 1)
    eng.tensor_tensor(t2, s[:, :, 2], s[:, :, 5], ALU.add).then_inc(step, 1)
    eng.wait_ge(step, k + 3)
    eng.tensor_scalar(mean, t0, 0.5, None, ALU.mult).then_inc(step, 1)
    eng.scalar_tensor_tensor(t1, t1, 0.25, t1, ALU.mult, ALU.mult).then_inc(step, 1)
    eng.wait_ge(step, k + 5)
    eng.scalar_tensor_tensor(t2, t2, 1.0 / 128, t1, ALU.mult, ALU.add).then_inc(step, 1)
    eng.wait_ge(step, k + 6)
    eng.tensor_scalar(var, t2, eps, None, ALU.add).then_inc(done, 1)


def block_kernel(nc, x, wqT, wkT, wvT, wq2, wk2, wv2, wo, bq, bk, bv, bq2, bk2, bv2, bo, gamma, beta,
                 wgT, shared_w, expert_w, ident_d, upper_d, before_d, slot_d, cols_d, block4_d, jrow_d,
                 earlier_d, head_d, out):
    fp32, fp16, bf16, i32 = mybir.dt.float32, mybir.dt.float16, mybir.dt.bfloat16, mybir.dt.int32
    ALU, ACT, AX = mybir.AluOpType, mybir.ActivationFunctionType, mybir.AxisListType

    P = 128
    B, L, D = x.shape
    T = B * L
    NT = T // P
    TB = L // P
    E = wgT.shape[1]
    M = 4
    NG = E // M
    CAP, TOPK = 160, 8
    REST = CAP - P
    FC = expert_w.shape[2] // P // 3
    ROW = D + E
    H, DH = 16, D // 16
    NGP = NG + 2
    EPS_LN, EPS_ATT, EPS_QK = 1e-5, 1e-3, 1e-6
    F32_EPS = 1.1920929e-07
    NC_X = 4
    TC = NT // NC_X
    assert NG == B and M * NT == P and P + REST == CAP

    ctx = ExitStack()
    with ctx:
        def sb(name, shape, dt=fp32):
            return ctx.enter_context(nc.sbuf_tensor(name, shape, dt))

        def sem(name):
            return ctx.enter_context(nc.semaphore(name))

        def dram(name, shape, dt=fp32):
            return nc.dram_tensor(name, shape, dt, kind="Internal").ap()

        xng = dram("xng", [T + P, ROW])
        xT_d = dram("xT_d", [B, P, L])
        cum_d = dram("cum_d", [E, NT, P], fp16)
        acc_d = [dram(f"acc_d{i}", [T + P, D]) for i in range(2)]

        ident = sb("ident", [P, P])
        upper_f, upper = sb("upper_f", [P, P]), sb("upper", [P, P], bf16)
        before_f, before = sb("before_f", [P, P]), sb("before", [P, P], fp16)
        slot_f, slot = sb("slot_f", [P, CAP]), sb("slot", [P, CAP], fp16)
        cols = sb("cols", [P, 8])
        block4 = sb("block4", [P, M])
        jrow = sb("jrow", [P, M + 1])
        earlier, head = sb("earlier", [P, P]), sb("head", [P, P])
        ones, half = sb("ones", [P, P]), sb("half", [P, 8])
        zeros = sb("zeros", [P, 1024])
        wqT_s, wkT_s, wvT_s = sb("wqT_s", [P, D]), sb("wkT_s", [P, D]), sb("wvT_s", [P, D])
        w2_s = sb("w2_s", [P, 3, D])
        wo_s, wg_s = sb("wo_s", [P, D]), sb("wg_s", [P, E])
        bcol = sb("bcol", [P, 4])
        brow = sb("brow", [P, 2, D])
        bo_b, gamma_b, beta_b = sb("bo_b", [P, D]), sb("gamma_b", [P, D]), sb("beta_b", [P, D])
        brep = sb("brep", [P, 2, P])
        wqk = sb("wqk", [P, 2 * D])
        wv = sb("wv", [P, D])
        bqk1 = sb("bqk1", [P, 2 * D])
        bvc = sb("bvc", [P, 1])
        shw = sb("shw", [P, 9 * P])
        x_sb = sb("x_sb", [P, NT, D])
        xnb = sb("xnb", [P, NT, D])
        st = sb("st", [P, NT, 6])
        mean, var, rstd = sb("mean", [P, NT]), sb("var", [P, NT]), sb("rstd", [P, NT])
        m_t = sb("m_t", [P, 4, TC])
        xm = sb("xm", [P, TB, D])
        xn = sb("xn", [P, 2, TB, D])
        xT = sb("xT", [P, 2, L])
        nmax, esum = sb("nmax", [P, 2, TB]), sb("esum", [P, 2, TB])
        ex = sb("ex", [P, 2, TB, E])
        top = sb("top", [P, 2, TB, TOPK])
        left = sb("left", [P, 2, TB, E])
        mask = sb("mask", [P, 2, TB, E], bf16)
        tsum, rs, den, wt = (sb(n, [P, 2, TB]) for n in ("tsum", "rs", "den", "wt"))
        gw = sb("gw", [P, 2, TB, E])
        cum = sb("cum", [E, 2, TB, P], fp16)
        cumL = sb("cumL", [P, NGP, P], fp16)
        cumR = sb("cumR", [P, NGP, M, P], fp16)
        cnt_f = sb("cnt_f", [P, NGP])
        base, nxt = sb("base", [P, NGP]), sb("nxt", [P, NGP])
        jb = sb("jb", [P, NGP, M + 1, 2], fp16)
        ge, oh = sb("ge", [P, CAP], fp16), sb("oh", [P, CAP], fp16)
        ohr = sb("ohr", [P, M, REST], fp16)
        thr, cnt, tok, hit = (sb(n, [P, M + 1]) for n in ("thr", "cnt", "tok", "hit"))
        le = sb("le", [P, M + 1, P], fp16)
        v_all = sb("v_all", [P, NGP, M + 1])
        idx_all = sb("idx_all", [P, NGP, M + 1], i32)
        idx_g, idx_s = sb("idx_g", [P, M + 1], i32), sb("idx_s", [P, M + 1], i32)
        gath = sb("gath", [P, M + 1, ROW])
        ew = [sb(f"ew{m}", [P, 9 * P]) for m in range(M)]
        xe = sb("xe", [P, M, CAP])
        si, ac = sb("si", [P, 2, FC, CAP]), sb("ac", [P, 2, FC, CAP])
        wr_t, wrest = sb("wr_t", [P, M]), sb("wrest", [P, 1])
        ys = sb("ys", [P, M + 2, D])
        vrep, eq, dup_t = sb("vrep", [P, P]), sb("eq", [P, P]), sb("dup_t", [P, P])
        dup, first, vr = sb("dup", [P, 1]), sb("first", [P, 1]), sb("vr", [P, 1])
        xTb = sb("xTb", [P, L])
        u1, eu, f = (sb(n, [P, TB, 2 * D]) for n in ("u1", "eu", "f"))
        vT = sb("vT", [P, L])
        S_s, qk = sb("S_s", [P, D]), sb("qk", [P, TB, D])
        qks, rq = sb("qks", [P, TB, H]), sb("rq", [P, TB, H])
        o_s, oT_s, y = sb("o_s", [P, TB, D]), sb("oT_s", [P, L]), sb("y", [P, TB, D])
        st2, m2 = sb("st2", [P, TB, 6]), sb("m2", [P, 6, TB])
        yg = sb("yg", [P, TB, D])

        bank = [ctx.enter_context(nc.psum_tensor(f"bank{i}", [P, 512], fp32)) for i in range(8)]

        (s_const, s_w, s_x0, s_x1, s_x2, s_x3) = (sem(n) for n in
            ("const_in", "attw_in", "x_in0", "x_in1", "x_in2", "x_in3"))
        x_in = [s_x0, s_x1, s_x2, s_x3]
        cast_done, set_done, half_done = sem("cast_done"), sem("set_done"), sem("half_done")
        zero_out, zdone = sem("zero_out"), sem("zdone")
        fold_mm, fold_done = sem("fold_mm"), sem("fold_done")
        stat_d, var_ready, rstd_ready = sem("stat_d"), sem("var_ready"), sem("rstd_ready")
        xm_ready, xn_ready, xb_ready = sem("xm_ready"), sem("xn_ready"), sem("xb_ready")
        xn_out = [sem(f"xn_out{s}") for s in range(2)]
        xTp_ready, xT_ready = sem("xTp_ready"), sem("xT_ready")
        xT_out = [sem(f"xT_out{s}") for s in range(2)]
        logit_ready, nmax_ready, ex_ready = sem("logit_ready"), sem("nmax_ready"), sem("ex_ready")
        top_ready, left_ready, mask_ready = sem("top_ready"), sem("left_ready"), sem("mask_ready")
        gate_c, wt_c, gw_ready, wrest_c = sem("gate_c"), sem("wt_c"), sem("gw_ready"), sem("wrest_c")
        h2_ready = sem("h2_ready")
        waited, waited_sp = sem("waited"), sem("waited_sp")
        gw_out = [sem(f"gw_out{s}") for s in range(2)]
        cump_ready, cum_ready = sem("cump_ready"), sem("cum_ready")
        cum_out = [sem(f"cum_out{s}") for s in range(2)]
        cum_in, tab_zero, cntf_done = sem("cum_in"), sem("tab_zero"), sem("cntf_done")
        base_mm, base_done, jb_done = sem("base_mm"), sem("base_done"), sem("jb_done")
        oh_ready, tab_mm, tab_step, idx_ready = (sem(n) for n in ("oh_ready", "tab_mm", "tab_step", "idx_ready"))
        idxg_c, idxs_c = sem("idxg_copied"), sem("idxs_copied")
        g_in = [sem(f"gathered{m}") for m in range(M + 1)]
        w_in = [sem(f"expert_in{m}") for m in range(M)]
        s_shw = sem("shared_in")
        xeP, xe_done, wrest_done = sem("xe_psum"), sem("xe_done"), sem("wrest_done")
        h_ready, si_ready, ac_ready, y_ready, y_used = (sem(n) for n in
            ("h_ready", "silu_ready", "act_ready", "y_ready", "y_used"))
        ys_ready, s_sc = sem("ys_ready"), [sem(f"scattered{m}") for m in range(M + 1)]
        vrep_ready, eq_step, idxs_ready, sum_mm, ysum_ready = (sem(n) for n in
            ("vrep_ready", "eq_step", "idxrest_ready", "sum_mm", "ysum_ready"))
        xTb_in = sem("xTb_in")
        qk_ready, v_ready, u_ready, eu_ready, f_ready, vT_done = (sem(n) for n in
            ("qk_ready", "v_ready", "u_ready", "eu_ready", "f_ready", "vT_done"))
        S_ready, Ss_done, qks_step, rq_ready, o_ready, o_done = (sem(n) for n in
            ("S_ready", "S_masked", "qks_step", "rq_ready", "o_ready", "o_done"))
        oTp_ready, oT_done, z_ready, z_used = (sem(n) for n in ("oTp_ready", "oT_done", "z_ready", "z_used"))
        y_step, v2_ready, r2_ready, res_step = (sem(n) for n in ("y_step", "var2_ready", "rstd2_ready", "res_step"))
        acc_in = [sem(f"acc_in{c}") for c in range(NC_X)]
        fin_step, fin_ready, out_sem = sem("fin_step"), sem("fin_ready"), sem("out_done")

        block = ctx.enter_context(nc.Block())

        xr = x.rearrange("b (j p) d -> p (b j) d", p=P)
        xng_x = xng[0:T, 0:D].rearrange("(b j p) d -> b p j d", p=P, j=TB)
        xng_g = xng[0:T, D:ROW].rearrange("(b j p) d -> b p j d", p=P, j=TB)
        cum_st = cum_d.rearrange("e (b j) t -> b e j t", j=TB)
        outr = out.rearrange("(n p) d -> p n d", p=P)
        accr = [a[0:T, :].rearrange("(n p) d -> p n d", p=P) for a in acc_d]
        Y, R, X, A = (bank[3], bank[4]), bank[5], bank[6], bank[7]
        UNITS = 2 + M
        NCONST, NATT_IN, NZERO = 9, 17, 11
        ORDER_G = (M, 0, 1, 2, 3)
        cumR_f = cumR[:, :, :, :].rearrange("p q m t -> p (q m t)").bitcast(fp32)[:, 0:T].rearrange(
            "p (n d) -> p n d", d=D)

        def hview(u, which, n):
            return bank[(2 * u + 1 - which) % 3][:, 0:FC * n].rearrange("p (c n) -> p c n", c=FC)

        @block.sync
        def _(sp):
            for c in range(NC_X):
                sp.dma_start(x_sb[:, c * TC:(c + 1) * TC, :], xr[:, c * TC:(c + 1) * TC, :]).then_inc(x_in[c], 16)
            for dst, src in ((ident, ident_d), (upper_f, upper_d), (before_f, before_d), (slot_f, slot_d),
                             (cols, cols_d), (block4, block4_d), (jrow, jrow_d), (earlier, earlier_d),
                             (head, head_d)):
                sp.dma_start(dst[:, :], src).then_inc(s_const, 16)
            for dst, src in ((wqT_s[:, :], wqT), (wkT_s[:, :], wkT), (wvT_s[:, :], wvT),
                             (w2_s[:, 0, :], wq2), (w2_s[:, 1, :], wk2), (w2_s[:, 2, :], wv2),
                             (wo_s[:, :], wo), (wg_s[:, :], wgT),
                             (bcol[:, 0:1], bq.rearrange("(p a) -> p a", a=1)),
                             (bcol[:, 1:2], bk.rearrange("(p a) -> p a", a=1)),
                             (bcol[:, 2:3], bv.rearrange("(p a) -> p a", a=1)),
                             (bcol[:, 3:4], bv2.rearrange("(p a) -> p a", a=1)),
                             (brow[:, 0, :], bq2.partition_broadcast(P)),
                             (brow[:, 1, :], bk2.partition_broadcast(P)),
                             (bo_b[:, :], bo.partition_broadcast(P)),
                             (gamma_b[:, :], gamma.partition_broadcast(P)),
                             (beta_b[:, :], beta.partition_broadcast(P))):
                sp.dma_start(dst, src).then_inc(s_w, 16)
            sp.dma_start(shw[:, :], shared_w).then_inc(s_shw, 16)
            for m in range(M):
                sp.dma_start(ew[m][:, :], expert_w[m, :, :]).then_inc(w_in[m], 16)

            def batches(i):
                for s in range(2):
                    b = 2 * i + s
                    sp.wait_ge(xn_ready, b + 1)
                    sp.sem_inc(waited_sp, 1)
                    sp.dma_start(xng_x[b, :, :, :], xn[:, s, :, :]).then_inc(xn_out[s], 16)
                    sp.wait_ge(xT_ready, b + 1)
                    sp.sem_inc(waited_sp, 1)
                    sp.dma_start(xT_d[b, :, :], xT[:, s, :]).then_inc(xT_out[s], 16)
                for s in range(2):
                    b = 2 * i + s
                    sp.wait_ge(gw_ready, b + 1)
                    sp.sem_inc(waited_sp, 1)
                    sp.dma_start(xng_g[b, :, :, :], gw[:, s, :, :]).then_inc(gw_out[s], 16)
                    sp.wait_ge(cum_ready, b + 1)
                    sp.sem_inc(waited_sp, 1)
                    sp.dma_start(cum_st[b, :, :, :], cum[:, s, :, :]).then_inc(cum_out[s], 16)
            batches(0)
            with sp.Fori(1, B // 2) as i:
                batches(i)
            for s in range(2):
                sp.wait_ge(cum_out[s], 16 * B // 2)
                sp.wait_ge(xT_out[s], 16 * B // 2)
            sp.wait_ge(tab_zero, 2)
            for m in range(M):
                src = cum_d.rearrange("(q m) j t -> m j q t", m=M)[m, :, :, :]
                sp.dma_start(cumL[32 * m:32 * m + 32, 0:NG, :], src).then_inc(cum_in, 16)
                sp.dma_start(cumR[32 * m:32 * m + 32, 0:NG, m, :], src).then_inc(cum_in, 16)

            def loads(g):
                sp.wait_ge(h_ready, UNITS * g + 2)
                sp.sem_inc(waited_sp, 1)
                sp.wait_ge(v_ready, g + 1)
                sp.sem_inc(waited_sp, 1)
                sp.dma_start(xTb[:, :], xT_d[g + 1, :, :]).then_inc(xTb_in, 16)
                for m in range(M):
                    sp.wait_ge(y_ready, UNITS * g + 3 + m)
                    sp.sem_inc(waited_sp, 1)
                    sp.dma_start(ew[m][:, :], expert_w[M * g + M + m, :, :]).then_inc(w_in[m], 16)

            sp.dma_start(xTb[:, :], xT_d[0, :, :]).then_inc(xTb_in, 16)
            loads(0)
            with sp.Fori(1, NG - 1) as g:
                loads(g)

            for m in range(M + 1):
                sp.wait_ge(s_sc[m], 16 * NG)
            sp.wait_ge(res_step, 5 * NG)
            for c in range(NC_X):
                n = slice(c * TC, (c + 1) * TC)
                sp.dma_start(xnb[:, n, :], accr[0][:, n, :]).then_inc(acc_in[c], 16)
                sp.dma_start(cumR_f[:, n, :], accr[1][:, n, :]).then_inc(acc_in[c], 16)
            for c in range(NC_X):
                n = slice(c * TC, (c + 1) * TC)
                sp.wait_ge(fin_ready, c + 1)
                sp.dma_start(outr[:, n, :], x_sb[:, n, :]).then_inc(out_sem, 16)
            sp.wait_ge(out_sem, 16 * NC_X)

        @block.gpsimd
        def _(pool):
            pool.memset(half[:, :], -0.5).then_inc(half_done, 1)
            for c in range(NC_X):
                n = slice(c * TC, (c + 1) * TC)
                pool.wait_ge(half_done, 1)
                pool.wait_ge(var_ready, c + 1)
                pool.tensor_tensor(rstd[:, n], var[:, n], half[:, 0:TC], ALU.pow).then_inc(rstd_ready, 1)
            pool.wait_ge(rstd_ready, NC_X)
            pool.wait_ge(s_w, 16 * NATT_IN)
            def batches(i):
                for s in range(2):
                    b = 2 * i + s
                    xb = x_sb[:, bass.ds(2 * b, TB), :]
                    pool.wait_ge(xn_ready, b)
                    pool.tensor_tensor(xm[:, :, :], xb, mean[:, bass.ds(2 * b, TB)].unsqueeze(2).to_broadcast([P, TB, D]),
                                       ALU.subtract).then_inc(xm_ready, 1)
                    pool.wait_ge(xm_ready, b + 1)
                    pool.wait_ge(xn_out[s], 16 * i)
                    pool.wait_ge(xTp_ready, 2 * i)
                    pool.tensor_tensor(xn[:, s, :, :], xm[:, :, :], rstd[:, bass.ds(2 * b, TB)].unsqueeze(2).to_broadcast([P, TB, D]),
                                       ALU.mult).then_inc(xn_ready, 1)
                    pool.tensor_tensor(xb, xb, beta_b[:, :].unsqueeze(1).to_broadcast([P, TB, D]), ALU.add).then_inc(xb_ready, 1)
                    pool.wait_ge(xn_ready, b + 1)
                    pool.tensor_tensor(xnb[:, bass.ds(2 * b, TB), :], xn[:, s, :, :],
                                       bo_b[:, :].unsqueeze(1).to_broadcast([P, TB, D]), ALU.add).then_inc(xb_ready, 1)
            batches(0)
            with pool.Fori(1, B // 2) as i:
                batches(i)
            pool.memset(cumL[:, :, :], 0.0).then_inc(tab_zero, 1)
            pool.memset(cumR[:, :, :, :], 0.0).then_inc(tab_zero, 1)
            for s in range(2):
                pool.wait_ge(xn_out[s], 16 * B // 2)
                pool.wait_ge(gw_out[s], 16 * B // 2)
            pool.wait_ge(zero_out, 16 * NZERO)

            def gather(g, m):
                pool.wait_ge(idx_ready, g + 1)
                pool.wait_ge(g_in[m], 16 * g)
                pool.sem_inc(waited, 1)
                pool.tensor_copy(idx_g[:, m:m + 1], idx_all[:, g, m:m + 1]).then_inc(idxg_c, 1)
                pool.wait_ge(idxg_c, (M + 1) * g + ORDER_G.index(m) + 1)
                pool.sem_inc(waited, 1)
                pool.indirect_dma_start(out=gath[:, m, :], out_offset=None, in_=xng,
                                        in_offset=bass.IndirectOffsetOnAxis(ap=idx_g[:, m:m + 1], axis=0)
                                        ).then_inc(g_in[m], 16)

            def scatter(g, m):
                acc = m % 2
                prev = {0: 4, 1: 3, 2: 0, 3: 1, 4: 2}[m]
                pool.wait_ge(s_sc[prev], 16 * (g + (1 if prev < m else 0)))
                pool.wait_ge(s_sc[m], 16 * g)
                if m < M:
                    pool.sem_inc(waited, 1)
                    pool.tensor_copy(idx_s[:, m:m + 1], idx_all[:, g, m:m + 1]).then_inc(idxs_c, 1)
                    pool.wait_ge(idxs_c, M * g + m + 1)
                    pool.wait_ge(ys_ready, (M + 1) * g + m + 1)
                    src = ys[:, m, :]
                else:
                    pool.wait_ge(idxs_ready, g + 1)
                    pool.wait_ge(ysum_ready, g + 1)
                    src = ys[:, M + 1, :]
                pool.sem_inc(waited, 1)
                pool.indirect_dma_start(out=acc_d[acc], out_offset=bass.IndirectOffsetOnAxis(ap=idx_s[:, m:m + 1], axis=0),
                                        in_=src, in_offset=None, compute_op=ALU.add).then_inc(s_sc[m], 16)

            def group(g, last):
                if not last:
                    pool.wait_ge(wrest_done, g + 1)
                    pool.wait_ge(xeP, (M + 1) * g + 2)
                    gather(g + 1, M)
                for m in range(M):
                    if m == 2:
                        pool.wait_ge(v2_ready, g + 1)
                        pool.tensor_tensor(m2[:, 5, :], m2[:, 4, :], half[:, 0:TB], ALU.pow).then_inc(r2_ready, 1)
                    scatter(g, m)
                    if not last:
                        gather(g + 1, m)
                scatter(g, M)

            for m in ORDER_G:
                gather(0, m)
            group(0, False)
            with pool.Fori(1, NG - 1) as g:
                group(g, False)
            group(NG - 1, True)

        @block.scalar
        def _(act):
            act.wait_ge(zdone, 1)
            for a in acc_d:
                flat = a.rearrange("(p r) d -> p (r d)", p=P)
                for k in range(0, flat.shape[1], 1024):
                    n = min(1024, flat.shape[1] - k)
                    act.dma_start(flat[:, k:k + n], zeros[:, 0:n]).then_inc(zero_out, 16)
            act.dma_start(xng[T:T + P, :], zeros[:, 0:ROW]).then_inc(zero_out, 16)
            def batches(i):
                for s in range(2):
                    b = 2 * i + s
                    act.wait_ge(xTp_ready, b + 1)
                    act.wait_ge(logit_ready, 2 * i)
                    act.wait_ge(xT_out[s], 16 * i)
                    act.activation(xT[:, s, :], bank[s][:, 0:L], ACT.Copy).then_inc(xT_ready, 1)
                for s in range(2):
                    b = 2 * i + s
                    act.wait_ge(nmax_ready, b + 1)
                    act.wait_ge(gw_ready, 2 * i)
                    for j in range(TB):
                        act.activation(ex[:, s, j, :], bank[2 + s][:, j * E:(j + 1) * E], ACT.Exp,
                                       bias=nmax[:, s, j:j + 1], accum_out=esum[:, s, j:j + 1]).then_inc(ex_ready, 1)
                for s in range(2):
                    b = 2 * i + s
                    act.wait_ge(cump_ready, b + 1)
                    act.wait_ge(cum_out[s], 16 * i)
                    act.activation(cum[:, s, :, :], bank[4 + s][0:E, 0:L].rearrange("e (j t) -> e j t", j=TB),
                                   ACT.Copy).then_inc(cum_ready, 1)

            batches(0)
            with act.Fori(1, B // 2) as i:
                batches(i)
            def silu(g, u):
                n = CAP if u >= 2 else P
                act.wait_ge(h2_ready, UNITS * g + u + 1)
                act.activation(si[:, u % 2, :, 0:n], hview(u, 1, n), ACT.Silu).then_inc(si_ready, 1)

            def xe_copy(g, k):
                act.wait_ge(xeP, (M + 1) * g + max(k, 1) + 1)
                if k == 0:
                    act.wait_ge(h_ready, UNITS * g)
                    act.activation(xe[:, :, P:CAP], X[:, 0:P].rearrange("p (m r) -> p m r", m=M),
                                   ACT.Copy).then_inc(xe_done, 1)
                else:
                    r = 1 if k == 1 else 0
                    act.activation(xe[:, k - 1, 0:P], X[:, r * P:(r + 1) * P], ACT.Copy).then_inc(xe_done, 1)

            def group(g):
                act.wait_ge(u_ready, g + 1)
                act.wait_ge(f_ready, g)
                act.activation(eu[:, :, :], u1[:, :, :], ACT.Exp, bias=cols[:, 7:8]).then_inc(eu_ready, 1)
                silu(g, 0)
                xe_copy(g, 0)
                xe_copy(g, 1)
                silu(g, 1)
                act.wait_ge(v_ready, g + 1)
                act.wait_ge(o_ready, g)
                act.activation(vT[:, :], A[:, 0:L], ACT.Identity, bias=bvc[:, 0:1]).then_inc(vT_done, 1)
                xe_copy(g, 2)
                silu(g, 2)
                xe_copy(g, 3)
                silu(g, 3)
                xe_copy(g, 4)
                silu(g, 4)
                act.wait_ge(oTp_ready, g + 1)
                act.wait_ge(z_ready, g)
                act.activation(oT_s[:, :], A[:, 0:L], ACT.Copy).then_inc(oT_done, 1)
                silu(g, 5)

            group(0)
            with act.Fori(1, NG) as g:
                group(g)

        @block.vector
        def _(dve):
            dve.memset(ones[:, :], 1.0).then_inc(set_done, 1)
            dve.memset(zeros[:, :], 0.0).then_inc(zdone, 1)
            for c in range(NC_X):
                n = slice(c * TC, (c + 1) * TC)
                dve.wait_ge(x_in[c], 16)
                with dve.Fori(0, TC) as t:
                    dve.bn_stats(st[:, t + c * TC, :], x_sb[:, t + c * TC, :]).then_inc(stat_d, 1)
                k = TC * (c + 1) + 6 * c
                dve.wait_ge(stat_d, k)
                moments(dve, st[:, n, :], m_t, mean[:, n], var[:, n], stat_d, k, EPS_LN, var_ready)
            dve.wait_ge(s_const, 16 * NCONST)
            dve.tensor_copy(upper[:, :], upper_f[:, :]).then_inc(cast_done, 1)
            dve.tensor_copy(before[:, :], before_f[:, :]).then_inc(cast_done, 1)
            dve.tensor_copy(slot[:, :], slot_f[:, :]).then_inc(cast_done, 1)
            dve.wait_ge(s_w, 16 * NATT_IN)
            dve.wait_ge(set_done, 1)
            for k in range(2):
                dve.tensor_scalar(brep[:, k, :], ones[:, :], bcol[:, k:k + 1], None, ALU.mult).then_inc(cast_done, 1)
            def batches(i):
                for s in range(2):
                    b = 2 * i + s
                    dve.wait_ge(logit_ready, b + 1)
                    dve.wait_ge(ex_ready, 4 * i)
                    dve.tensor_reduce(nmax[:, s, :], bank[2 + s][:, 0:TB * E].rearrange("p (j e) -> p j e", j=TB),
                                      AX.X, ALU.max, negate=True).then_inc(nmax_ready, 1)
                for s in range(2):
                    b = 2 * i + s
                    dve.wait_ge(ex_ready, 2 * b + 2)
                    dve.reciprocal(rs[:, s, :], esum[:, s, :]).then_inc(gate_c, 1)
                    for j in range(TB):
                        dve.max(top[:, s, j, :], ex[:, s, j, :]).then_inc(top_ready, 1)
                    dve.wait_ge(top_ready, 2 * b + 2)
                    dve.tensor_reduce(tsum[:, s, :], top[:, s, :, :], AX.X, ALU.add).then_inc(gate_c, 1)
                    for j in range(TB):
                        dve.match_replace(left[:, s, j, :], top[:, s, j, :], ex[:, s, j, :], -1.0).then_inc(left_ready, 1)
                    dve.wait_ge(left_ready, 2 * b + 2)
                    dve.wait_ge(cump_ready, 2 * i)
                    dve.tensor_scalar(mask[:, s, :, :], left[:, s, :, :], 0.0, None, ALU.is_lt).then_inc(mask_ready, 1)
                    dve.wait_ge(gate_c, 4 * b + 2)
                    dve.tensor_tensor(den[:, s, :], tsum[:, s, :], rs[:, s, :], ALU.mult).then_inc(gate_c, 1)
                    dve.wait_ge(gate_c, 4 * b + 3)
                    dve.tensor_scalar(den[:, s, :], den[:, s, :], F32_EPS, None, ALU.max).then_inc(gate_c, 1)
                    dve.wait_ge(gate_c, 4 * b + 4)
                    dve.reciprocal(wt[:, s, :], den[:, s, :]).then_inc(wt_c, 1)
                    dve.wait_ge(wt_c, 2 * b + 1)
                    dve.tensor_tensor(wt[:, s, :], wt[:, s, :], rs[:, s, :], ALU.mult).then_inc(wt_c, 1)
                    dve.wait_ge(wt_c, 2 * b + 2)
                    dve.wait_ge(gw_out[s], 16 * i)
                    dve.tensor_tensor(gw[:, s, :, :], ex[:, s, :, :], wt[:, s, :].unsqueeze(2).to_broadcast([P, TB, E]),
                                      ALU.mult).then_inc(gw_ready, 1)
            batches(0)
            with dve.Fori(1, B // 2) as i:
                batches(i)
            dve.wait_ge(fold_mm, 1)
            dve.tensor_copy(wqk[:, :], bank[6][:, 0:2 * D]).then_inc(fold_done, 1)
            dve.tensor_copy(wv[:, :], bank[6][:, 2 * D:3 * D]).then_inc(fold_done, 1)
            dve.scalar_tensor_tensor(bqk1[:, :], bank[7][:, 0:2 * D], 1.0, brow[:, :, :].rearrange("p a n -> p (a n)"),
                                     ALU.add, ALU.add).then_inc(fold_done, 1)
            dve.tensor_tensor(bvc[:, :], bank[7][:, 2 * D:2 * D + 1], bcol[:, 3:4], ALU.add).then_inc(fold_done, 1)
            dve.wait_ge(cum_in, 16 * 2 * M)
            dve.tensor_copy(cnt_f[:, :], cumL[:, :, P - 1]).then_inc(cntf_done, 1)
            dve.wait_ge(base_mm, 1)
            dve.tensor_copy(base[:, :], bank[5][:, 0:NGP]).then_inc(base_done, 1)
            dve.wait_ge(cntf_done, 1)
            dve.tensor_tensor(nxt[:, :], bank[5][:, 0:NGP], cnt_f[:, :], ALU.add).then_inc(base_done, 1)
            dve.wait_ge(base_done, 2)
            for m in range(M):
                dve.tensor_scalar(jb[:, :, m, 1], base[:, :], block4[:, m:m + 1], None, ALU.mult).then_inc(jb_done, 1)
            dve.tensor_copy(jb[:, :, M, 1], base[:, :]).then_inc(jb_done, 1)
            dve.tensor_copy(jb[:, :, :, 0], jrow[:, :].unsqueeze(1).to_broadcast([P, NGP, M + 1])).then_inc(jb_done, 1)

            def table_hot(q):
                dve.wait_ge(tab_mm, q)
                dve.tensor_scalar(ge[:, :], slot[:, :], base[:, bass.ds(q, 1)], None, ALU.is_ge).then_inc(oh_ready, 1)
                dve.wait_ge(oh_ready, 3 * q + 1)
                dve.scalar_tensor_tensor(oh[:, :], slot[:, :], nxt[:, bass.ds(q, 1)], ge[:, :], ALU.is_lt, ALU.mult).then_inc(oh_ready, 1)
                dve.wait_ge(oh_ready, 3 * q + 2)
                dve.tensor_tensor(ohr[:, :, :], oh[:, P:CAP].unsqueeze(1).to_broadcast([P, M, REST]),
                                  block4[:, :].unsqueeze(2).to_broadcast([P, M, REST]), ALU.mult).then_inc(oh_ready, 1)

            def table_tokens(q):
                N = 8
                small = X[:, P:P + 10].rearrange("p (k a) -> p k a", a=2)
                dve.wait_ge(tab_mm, q + 1)
                dve.wait_ge(idx_ready, q)
                dve.tensor_tensor(thr[:, :], cols[:, 0:M + 1], small[:, :, 1], ALU.subtract).then_inc(tab_step, 1)
                dve.wait_ge(tab_step, N * q + 1)
                dve.tensor_tensor(le[:, 0:M, :], A[:, :].rearrange("p (m t) -> p m t", m=M),
                                  thr[:, 0:M].unsqueeze(2).to_broadcast([P, M, P]), ALU.is_le).then_inc(tab_step, 1)
                dve.tensor_scalar(le[:, M, :], X[:, 0:P], thr[:, M:M + 1], None, ALU.is_le).then_inc(tab_step, 1)
                dve.tensor_scalar(hit[:, :], small[:, :, 0], 0.0, None, ALU.is_gt).then_inc(tab_step, 1)
                dve.wait_ge(tab_step, N * q + 4)
                dve.tensor_reduce(cnt[:, :], le[:, :, :], AX.X, ALU.add).then_inc(tab_step, 1)
                dve.wait_ge(tab_step, N * q + 5)
                dve.scalar_tensor_tensor(tok[:, :], small[:, :, 0], float(P), cnt[:, :], ALU.mult, ALU.add).then_inc(tab_step, 1)
                dve.wait_ge(tab_step, N * q + 6)
                dve.scalar_tensor_tensor(tok[:, :], tok[:, :], cols[:, 6:7], hit[:, :], ALU.subtract, ALU.mult).then_inc(tab_step, 1)
                dve.wait_ge(tab_step, N * q + 7)
                dve.tensor_scalar(v_all[:, q, :], tok[:, :], cols[:, 5:6], None, ALU.add).then_inc(tab_step, 1)
                dve.wait_ge(tab_step, N * q + 8)
                dve.tensor_copy(idx_all[:, q, :], v_all[:, q, :]).then_inc(idx_ready, 1)

            def act_mul(g, u):
                n = CAP if u >= 2 else P
                dve.wait_ge(si_ready, UNITS * g + u + 1)
                dve.wait_ge(h_ready, UNITS * g + u + 1)
                if u >= 2:
                    dve.wait_ge(y_ready, UNITS * g + u - 1)
                else:
                    dve.wait_ge(y_ready, UNITS * g)
                dve.tensor_tensor(ac[:, u % 2, :, 0:n], si[:, u % 2, :, 0:n], hview(u, 0, n), ALU.mult).then_inc(ac_ready, 1)

            def y_copy(g, m):
                dve.wait_ge(y_ready, UNITS * g + 3 + m)
                dve.wait_ge(s_sc[m], 16 * g)
                r = m % 2
                dve.tensor_scalar(ys[:, m, :], Y[r][:, 0:P], gath[:, m, bass.ds(D + M * g + m, 1)],
                                  None, ALU.mult).then_inc(ys_ready, 1)

            def group(g):
                tiles = bass.ds(TB * g, TB)
                xg, xnbg = x_sb[:, tiles, :], xnb[:, tiles, :]
                dve.wait_ge(qk_ready, g + 1)
                dve.wait_ge(f_ready, g)
                dve.tensor_tensor(u1[:, :, :], A[:, :].rearrange("p (j n) -> p j n", j=TB),
                                  bqk1[:, :].unsqueeze(1).to_broadcast([P, TB, 2 * D]), ALU.add).then_inc(u_ready, 1)
                dve.wait_ge(g_in[M], 16 * g + 16)
                dve.wait_ge(idx_ready, g + 1)
                dve.tensor_tensor(wr_t[:, :], gath[:, M, bass.ds(D + M * g, M)], block4[:, :], ALU.mult).then_inc(wrest_c, 1)
                dve.tensor_scalar(vrep[:, :], ones[:, :], v_all[:, g, M:M + 1], None, ALU.mult).then_inc(vrep_ready, 1)
                dve.wait_ge(wrest_c, g + 1)
                dve.tensor_reduce(wrest[:, :], wr_t[:, :], AX.X, ALU.add).then_inc(wrest_done, 1)
                act_mul(g, 0)
                dve.wait_ge(eu_ready, g + 1)
                dve.wait_ge(S_ready, g)
                dve.scalar_tensor_tensor(f[:, :, :].rearrange("p j n -> p (j n)"), eu[:, :, :].rearrange("p j n -> p (j n)"), 1.0,
                                         u1[:, :, :].rearrange("p j n -> p (j n)"), ALU.min, ALU.max).then_inc(f_ready, 1)
                act_mul(g, 1)
                def shared_rows(k):
                    dve.wait_ge(y_ready, UNITS * g + 1 + k)
                    xt = x_sb[:, TB * g + k, :]
                    dve.tensor_tensor(xt, xt, Y[k][:, 0:P], ALU.add).then_inc(y_used, 1)
                shared_rows(0)
                dve.wait_ge(S_ready, g + 1)
                dve.tensor_tensor(S_s[:, :], R[:, 0:P], head[:, :], ALU.mult).then_inc(Ss_done, 1)
                dve.wait_ge(sum_mm, g)
                dve.tensor_scalar(eq[:, :], R[:, P:2 * P], v_all[:, g, M:M + 1], None, ALU.is_equal).then_inc(eq_step, 1)
                act_mul(g, 2)
                shared_rows(1)
                dve.wait_ge(f_ready, g + 1)
                dve.tensor_tensor(qk[:, :, :], f[:, :, 0:D], f[:, :, D:2 * D], ALU.mult).then_inc(qks_step, 1)
                dve.wait_ge(qks_step, 3 * g + 1)
                dve.tensor_reduce(qks[:, :, :], qk[:, :, :].rearrange("p j (h d) -> p j h d", h=H), AX.X, ALU.add).then_inc(qks_step, 1)
                dve.wait_ge(qks_step, 3 * g + 2)
                dve.tensor_scalar(qks[:, :, :], qks[:, :, :], EPS_QK, None, ALU.add).then_inc(qks_step, 1)
                dve.wait_ge(qks_step, 3 * g + 3)
                dve.reciprocal(rq[:, :, :], qks[:, :, :]).then_inc(rq_ready, 1)
                act_mul(g, 3)
                dve.wait_ge(o_ready, g + 1)
                dve.wait_ge(rq_ready, g + 1)
                dve.tensor_tensor(o_s[:, :, :].rearrange("p j (h d) -> p (j h) d", h=H),
                                  A[:, 0:TB * D].rearrange("p (n d) -> p n d", d=DH),
                                  rq[:, :, :].rearrange("p j h -> p (j h)").unsqueeze(2).to_broadcast([P, TB * H, DH]),
                                  ALU.mult).then_inc(o_done, 1)
                y_copy(g, 0)
                dve.wait_ge(eq_step, 5 * g + 1)
                dve.tensor_tensor(dup_t[:, :], eq[:, :], earlier[:, :], ALU.mult).then_inc(eq_step, 1)
                dve.wait_ge(eq_step, 5 * g + 2)
                dve.tensor_reduce(dup[:, :], dup_t[:, :], AX.X, ALU.add).then_inc(eq_step, 1)
                dve.wait_ge(eq_step, 5 * g + 3)
                dve.tensor_scalar(first[:, :], dup[:, :], 0.5, None, ALU.is_lt).then_inc(eq_step, 1)
                act_mul(g, 4)
                dve.wait_ge(eq_step, 5 * g + 4)
                dve.scalar_tensor_tensor(vr[:, :], v_all[:, g, M:M + 1], cols[:, 5:6], first[:, :], ALU.subtract, ALU.mult).then_inc(eq_step, 1)
                dve.wait_ge(eq_step, 5 * g + 5)
                dve.wait_ge(s_sc[M], 16 * g)
                dve.tensor_scalar(idx_s[:, M:M + 1], vr[:, :], cols[:, 5:6], None, ALU.add).then_inc(idxs_ready, 1)
                y_copy(g, 1)
                act_mul(g, 5)
                table_hot(g + 2)
                dve.wait_ge(z_ready, g + 1)
                dve.tensor_tensor(y[:, :, :], A[:, 0:TB * D].rearrange("p (j n) -> p j n", j=TB), xnbg, ALU.add).then_inc(z_used, 1)
                y_copy(g, 2)
                dve.wait_ge(z_used, g + 1)
                for j in range(TB):
                    dve.bn_stats(st2[:, j, :], y[:, j, :]).then_inc(y_step, 1)
                dve.wait_ge(y_step, 8 * g + 2)
                moments(dve, st2[:, :, :], m2, m2[:, 3, :], m2[:, 4, :], y_step, 8 * g + 2, EPS_ATT, v2_ready)
                y_copy(g, 3)
                dve.wait_ge(wrest_done, g + 1)
                dve.tensor_scalar(ys[:, M, :], R[:, 0:P], wrest[:, 0:1], None, ALU.mult).then_inc(ys_ready, 1)
                table_tokens(g + 2)
                for j in range(TB):
                    dve.scalar_tensor_tensor(yg[:, j, :], y[:, j, :], m2[:, 3, j:j + 1], gamma_b[:, :], ALU.subtract, ALU.mult).then_inc(res_step, 1)
                dve.wait_ge(res_step, 5 * g + 2)
                dve.wait_ge(r2_ready, g + 1)
                for j in range(TB):
                    dve.tensor_scalar(yg[:, j, :], yg[:, j, :], m2[:, 5, j:j + 1], None, ALU.mult).then_inc(res_step, 1)
                dve.wait_ge(sum_mm, g + 1)
                dve.wait_ge(s_sc[M], 16 * g)
                dve.tensor_copy(ys[:, M + 1, :], R[:, 0:P]).then_inc(ysum_ready, 1)
                dve.wait_ge(res_step, 5 * g + 4)
                dve.wait_ge(y_used, 2 * g + 2)
                dve.tensor_tensor(xg, xg, yg[:, :, :], ALU.add).then_inc(res_step, 1)

            dve.wait_ge(xb_ready, 2 * B)
            for q in range(2):
                table_hot(q)
                dve.wait_ge(jb_done, M + 2)
                table_tokens(q)
            group(0)
            with dve.Fori(1, NG) as g:
                group(g)

            for c in range(NC_X):
                n = slice(c * TC, (c + 1) * TC)
                dve.wait_ge(acc_in[c], 32)
                dve.tensor_tensor(xnb[:, n, :], xnb[:, n, :], cumR_f[:, n, :], ALU.add).then_inc(fin_step, 1)
                dve.wait_ge(fin_step, c + 1)
                dve.tensor_tensor(x_sb[:, n, :], x_sb[:, n, :], xnb[:, n, :], ALU.add).then_inc(fin_ready, 1)

        @block.tensor
        def _(pe):
            pe.wait_ge(s_w, 16 * NATT_IN)
            pe.matmul(bank[6][:, 0:D], wqT_s[:, :], w2_s[:, 0, :], start=True, stop=True)
            pe.matmul(bank[6][:, D:2 * D], wkT_s[:, :], w2_s[:, 1, :], start=True, stop=True)
            pe.matmul(bank[6][:, 2 * D:3 * D], wvT_s[:, :], w2_s[:, 2, :], start=True, stop=True)
            pe.wait_ge(cast_done, 5)
            for k in range(2):
                pe.matmul(bank[7][:, k * D:(k + 1) * D], brep[:, k, :], w2_s[:, k, :], start=True, stop=True)
            pe.matmul(bank[7][:, 2 * D:2 * D + 1], w2_s[:, 2, :], bcol[:, 2:3], start=True, stop=True).then_inc(fold_mm, 1)
            def batches(i):
                for s in range(2):
                    b = 2 * i + s
                    pe.wait_ge(xn_ready, b + 1)
                    pe.wait_ge(xT_ready, 2 * i)
                    for j in range(TB):
                        last = pe.transpose(bank[s][:, j * P:(j + 1) * P], xn[:, s, j, :], ident[:, :])
                    last.then_inc(xTp_ready, 1)
                for s in range(2):
                    b = 2 * i + s
                    pe.wait_ge(xT_ready, b + 1)
                    pe.wait_ge(ex_ready, 4 * i)
                    for j in range(TB):
                        last = pe.matmul(bank[2 + s][:, j * E:(j + 1) * E], xT[:, s, j * P:(j + 1) * P], wg_s[:, :], start=True, stop=True)
                    last.then_inc(logit_ready, 1)
                for s in range(2):
                    b = 2 * i + s
                    pe.wait_ge(mask_ready, b + 1)
                    pe.wait_ge(cum_ready, 2 * i)
                    for j in range(TB):
                        last = pe.matmul(bank[4 + s][0:E, j * P:(j + 1) * P], mask[:, s, j, :], upper[:, :], start=True, stop=True)
                    last.then_inc(cump_ready, 1)
            batches(0)
            with pe.Fori(1, B // 2) as i:
                batches(i)
            pe.wait_ge(cum_in, 16 * 2 * M)
            pe.wait_ge(fold_done, 4)
            pe.wait_ge(cum_ready, B)
            pe.matmul(bank[5][:, 0:NGP], before[:, :], cumL[:, :, P - 1], start=True, stop=True).then_inc(base_mm, 1)

            def table(q):
                pe.wait_ge(oh_ready, 3 * q + 3)
                pe.matmul(A[:, :], oh[:, 0:P], cumR[:, q, :, :].rearrange("p m t -> p (m t)"), start=True, stop=True)
                pe.matmul(X[:, P:P + 8], oh[:, 0:P], jb[:, q, 0:M, :].rearrange("p m a -> p (m a)"), start=True, stop=True)
                pe.matmul(X[:, 0:P], ohr[:, :, :].rearrange("p m r -> p (m r)"), cumL[:, q, :], start=True, stop=True)
                pe.matmul(X[:, P + 8:P + 10], ohr[:, :, :].rearrange("p m r -> p (m r)"), jb[:, q, M, :], start=True, stop=True).then_inc(tab_mm, 1)

            def up(g, u):
                w = shw if u < 2 else ew[u - 2]
                pe.wait_ge(ac_ready, UNITS * g + max(u - 1, 0))
                if u >= 2:
                    pe.wait_ge(xe_done, (M + 1) * g + u)
                    pe.wait_ge(w_in[u - 2], 16 * g + 16)
                    rhs = xe[:, u - 2, :]
                else:
                    rhs = xTb[:, u * P:(u + 1) * P]
                n = CAP if u >= 2 else P
                for half_ in (1, 0):
                    if half_ == 0:
                        pe.wait_ge(si_ready, UNITS * g + u)
                    for c in range(FC):
                        k = half_ * FC + c
                        last = pe.matmul(hview(u, half_, n)[:, c, :], w[:, k * P:(k + 1) * P], rhs, start=True, stop=True)
                    last.then_inc(h2_ready if half_ else h_ready, 1)

            def down(g, u):
                w = shw if u < 2 else ew[u - 2]
                pe.wait_ge(ac_ready, UNITS * g + u + 1)
                r = u % 2
                if u < 2:
                    pe.wait_ge(ys_ready, (M + 1) * g)
                elif u < 4:
                    pe.wait_ge(y_used, 2 * g + u - 1)
                else:
                    pe.wait_ge(ys_ready, (M + 1) * g + u - 3)
                for c in range(FC):
                    last = pe.matmul(Y[r][:, 0:P], ac[:, r, c, 0:P], w[:, (6 + c) * P:(7 + c) * P],
                                     start=(c == 0), stop=(c == FC - 1))
                if u >= 2:
                    m = u - 2
                    if m == 0:
                        pe.wait_ge(Ss_done, g + 1)
                        pe.wait_ge(eq_step, 5 * g + 1)
                    for c in range(FC):
                        last = pe.matmul(R[32 * m:32 * m + 32, 0:P], ac[:, r, c, P:CAP], w[:, (6 + c) * P:(7 + c) * P],
                                         start=(c == 0), stop=(c == FC - 1))
                last.then_inc(y_ready, 1)

            def rows_T(g, k):
                if k == 1:
                    pe.wait_ge(g_in[M], 16 * g + 16)
                    pe.wait_ge(g_in[0], 16 * g + 16)
                    pe.transpose(X[:, 0:P], gath[:, M, 0:D], ident[:, :])
                    pe.transpose(X[:, P:2 * P], gath[:, 0, 0:D], ident[:, :]).then_inc(xeP, 2)
                else:
                    pe.wait_ge(g_in[k - 1], 16 * g + 16)
                    pe.wait_ge(xe_done, (M + 1) * g + k)
                    pe.transpose(X[:, 0:P], gath[:, k - 1, 0:D], ident[:, :]).then_inc(xeP, 1)

            def group(g):
                pe.wait_ge(xTb_in, 16 * g + 16)
                pe.wait_ge(idx_ready, g + 2)
                for j in range(TB):
                    last = pe.matmul(A[:, j * 2 * D:(j + 1) * 2 * D], xTb[:, j * P:(j + 1) * P], wqk[:, :], start=True, stop=True)
                last.then_inc(qk_ready, 1)
                up(g, 0)
                rows_T(g, 1)
                up(g, 1)
                pe.wait_ge(u_ready, g + 1)
                pe.matmul(A[:, 0:L], wv[:, :], xTb[:, :], start=True, stop=True).then_inc(v_ready, 1)
                down(g, 0)
                rows_T(g, 2)
                pe.wait_ge(f_ready, g + 1)
                pe.wait_ge(ysum_ready, g)
                for j in range(TB):
                    last = pe.matmul(R[:, 0:P], f[:, j, D:2 * D], f[:, j, 0:D], start=(j == 0), stop=(j == TB - 1))
                pe.wait_ge(vrep_ready, g + 1)
                pe.transpose(R[:, P:2 * P], vrep[:, :], ident[:, :]).then_inc(S_ready, 1)
                up(g, 2)
                down(g, 1)
                rows_T(g, 3)
                up(g, 3)
                pe.wait_ge(Ss_done, g + 1)
                pe.wait_ge(vT_done, g + 1)
                for j in range(TB):
                    last = pe.matmul(A[:, j * D:(j + 1) * D], vT[:, j * P:(j + 1) * P], S_s[:, :], start=True, stop=True)
                last.then_inc(o_ready, 1)
                down(g, 2)
                rows_T(g, 4)
                up(g, 4)
                down(g, 3)
                pe.wait_ge(o_done, g + 1)
                for j in range(TB):
                    last = pe.transpose(A[:, j * P:(j + 1) * P], o_s[:, j, :], ident[:, :])
                last.then_inc(oTp_ready, 1)
                up(g, 5)
                down(g, 4)
                pe.wait_ge(oT_done, g + 1)
                for j in range(TB):
                    last = pe.matmul(A[:, j * D:(j + 1) * D], oT_s[:, j * P:(j + 1) * P], wo_s[:, :], start=True, stop=True)
                last.then_inc(z_ready, 1)
                down(g, 5)
                pe.wait_ge(z_used, g + 1)
                pe.wait_ge(xe_done, (M + 1) * (g + 1))
                table(g + 2)
                pe.wait_ge(ys_ready, (M + 1) * g + M + 1)
                pe.matmul(R[:, 0:P], eq[:, :], ys[:, M, :], start=True, stop=True).then_inc(sum_mm, 1)

            pe.wait_ge(jb_done, M + 2)
            table(0)
            pe.wait_ge(idx_ready, 1)
            table(1)
            pe.wait_ge(s_shw, 16)
            group(0)
            with pe.Fori(1, NG) as g:
                group(g)


_VECTORS = ['bq', 'bk', 'bv', 'bq2', 'bk2', 'bv2', 'bo', 'gamma', 'beta']


def kernel(**inputs):
    import numpy as _np
    import concourse.bacc as _bacc
    from concourse import mybir as _mybir
    from concourse.bass_utils import run_bass_kernel_spmd as _run

    a = {n: _np.asarray(v) for n, v in inputs.items()}
    P, M = 128, 4
    x = a['L0_attn_x']
    B, L, D = x.shape
    NT = B * L // P

    def packed(w1, w2):
        up = _np.swapaxes(w1, -1, -2)
        down = _np.swapaxes(w2, -1, -2)
        c = down.shape[-2] // P
        down = down.reshape(down.shape[:-2] + (c, P, D))
        down = _np.swapaxes(down, -3, -2).reshape(down.shape[:-3] + (P, c * D))
        return _np.concatenate([up, down], axis=-1)

    arrays = {'x': x}
    for n in ('Wq', 'Wk', 'Wv'):
        arrays[n + 'T'] = a['L0_attn_' + n].T
    for n in ('Wq2', 'Wk2', 'Wv2', 'Wo'):
        arrays[n] = a['L0_attn_' + n]
    for n in _VECTORS:
        arrays[n] = a['L0_attn_' + n]
    arrays['wgT'] = a['L0_ffn_wg'].T
    arrays['shared_w'] = packed(a['L0_ffn_shared_w1'], a['L0_ffn_shared_w2'])
    arrays['expert_w'] = packed(a['L0_ffn_expert_w1'], a['L0_ffn_expert_w2'])

    p = _np.arange(P)
    row, col = p[:, None], p[None, :]
    rest = P + p % 32
    cols = _np.stack([p, p, p, p, rest, B * L + p, B * L + p + P, -_np.ones(P)], axis=1)
    block4 = (row // 32 == _np.arange(M)[None, :])
    jrow = _np.concatenate([block4 * (row % 32 + 1), row % 32 + 1], axis=1)
    constants = {
        'ident': row == col,
        'upper': row <= col,
        'before': (row // 32 == col // 32) & (row < col),
        'slots': _np.broadcast_to(_np.arange(160)[None, :], (P, 160)),
        'cols': cols,
        'block4': block4,
        'jrow': jrow,
        'earlier': col < row,
        'head': row // 8 == col // 8,
    }
    for n, v in constants.items():
        arrays['c_' + n] = v.astype(_np.float32)

    nc = _bacc.Bacc("TRN2", target_bir_lowering=False, num_devices=1)
    given, args = {}, []
    for n, v in arrays.items():
        v = _np.ascontiguousarray(v)
        given[f"in_{n}"] = v
        args.append(nc.dram_tensor(f"in_{n}", v.shape, _mybir.dt.from_np(v.dtype), kind="ExternalInput").ap())
    args.append(nc.dram_tensor("out_0", (B * L, D), _mybir.dt.float32, kind="ExternalOutput").ap())
    block_kernel(nc, *args)
    r = _run(nc, [given], core_ids=[0])
    return r.results[0]["out_0"].reshape(B, L, D)
```

```python
import concourse.bass as bass
from concourse import mybir
from contextlib import ExitStack



def since(count):
    return max(count, 0) if isinstance(count, int) else count


def moments(eng, s, t, mean, var, step, k, eps, done):
    ALU = mybir.AluOpType
    t0, t1, t2 = t[:, 0, :], t[:, 1, :], t[:, 2, :]
    eng.tensor_tensor(t0, s[:, :, 1], s[:, :, 4], ALU.add).then_inc(step, 1)
    eng.tensor_tensor(t1, s[:, :, 1], s[:, :, 4], ALU.subtract).then_inc(step, 1)
    eng.tensor_tensor(t2, s[:, :, 2], s[:, :, 5], ALU.add).then_inc(step, 1)
    eng.wait_ge(step, k + 3)
    eng.tensor_scalar(mean, t0, 0.5, None, ALU.mult).then_inc(step, 1)
    eng.scalar_tensor_tensor(t1, t1, 0.25, t1, ALU.mult, ALU.mult).then_inc(step, 1)
    eng.wait_ge(step, k + 5)
    eng.scalar_tensor_tensor(t2, t2, 1.0 / 128, t1, ALU.mult, ALU.add).then_inc(step, 1)
    eng.wait_ge(step, k + 6)
    eng.tensor_scalar(var, t2, eps, None, ALU.add).then_inc(done, 1)


def block_kernel(nc, x, wqT, wkT, wvT, wq2, wk2, wv2, wo, bq, bk, bv, bq2, bk2, bv2, bo, gamma, beta,
                 wgT, shared_w, expert_w, ident_d, upper_d, before_d, slot_d, cols_d, block4_d, jrow_d,
                 earlier_d, head_d, out):
    fp32, fp16, bf16, i32 = mybir.dt.float32, mybir.dt.float16, mybir.dt.bfloat16, mybir.dt.int32
    ALU, ACT, AX = mybir.AluOpType, mybir.ActivationFunctionType, mybir.AxisListType

    P = 128
    B, L, D = x.shape
    T = B * L
    NT = T // P
    TB = L // P
    E = wgT.shape[1]
    M = 4
    NG = E // M
    CAP, TOPK = 160, 8
    REST = CAP - P
    FC = expert_w.shape[2] // P // 3
    ROW = D + E
    H, DH = 16, D // 16
    NGP = NG + 1
    EPS_LN, EPS_ATT, EPS_QK = 1e-5, 1e-3, 1e-6
    F32_EPS = 1.1920929e-07
    NC_X = 4
    TC = NT // NC_X
    assert NG == B and M * NT == P and P + REST == CAP

    ctx = ExitStack()
    with ctx:
        def sb(name, shape, dt=fp32):
            return ctx.enter_context(nc.sbuf_tensor(name, shape, dt))

        def sem(name):
            return ctx.enter_context(nc.semaphore(name))

        def dram(name, shape, dt=fp32):
            return nc.dram_tensor(name, shape, dt, kind="Internal").ap()

        xng = dram("xng", [T + P, ROW])
        cum_d = dram("cum_d", [E, NT, P], fp16)
        acc = dram("acc", [T + P, D])

        ident = sb("ident", [P, P])
        upper_f, upper = sb("upper_f", [P, P]), sb("upper", [P, P], bf16)
        before_f, before = sb("before_f", [P, P]), sb("before", [P, P], fp16)
        slot_f, slot = sb("slot_f", [P, CAP]), sb("slot", [P, CAP], fp16)
        cols = sb("cols", [P, 8])
        block4 = sb("block4", [P, M])
        jrow = sb("jrow", [P, M + 1])
        earlier, head = sb("earlier", [P, P]), sb("head", [P, P])
        ones, half = sb("ones", [P, P]), sb("half", [P, 8])
        zeros = sb("zeros", [P, 1024])
        wqT_s, wkT_s, wvT_s = sb("wqT_s", [P, D]), sb("wkT_s", [P, D]), sb("wvT_s", [P, D])
        w2_s = sb("w2_s", [P, 3, D])
        wo_s, wg_s = sb("wo_s", [P, D]), sb("wg_s", [P, E])
        bcol = sb("bcol", [P, 4])
        brow = sb("brow", [P, 2, D])
        bo_b, gamma_b, beta_b = sb("bo_b", [P, D]), sb("gamma_b", [P, D]), sb("beta_b", [P, D])
        brep = sb("brep", [P, 2, P])
        wqk = sb("wqk", [P, 2 * D])
        wv = sb("wv", [P, D])
        bqk1 = sb("bqk1", [P, 2 * D])
        bvc = sb("bvc", [P, 1])
        shw = sb("shw", [P, 9 * P])
        x_sb = sb("x_sb", [P, NT, D])
        xnb = sb("xnb", [P, NT, D])
        st = sb("st", [P, NT, 6])
        mean, var, rstd = sb("mean", [P, NT]), sb("var", [P, NT]), sb("rstd", [P, NT])
        m_t = sb("m_t", [P, 4, TC])
        xm = sb("xm", [P, TB, D])
        xn = sb("xn", [P, 2, TB, D])
        xT = sb("xT", [P, 2, L])
        nmax, esum = sb("nmax", [P, 2, TB]), sb("esum", [P, 2, TB])
        ex = sb("ex", [P, 2, TB, E])
        top = sb("top", [P, 2, TB, TOPK])
        left = sb("left", [P, 2, TB, E])
        mask = sb("mask", [P, 2, TB, E], bf16)
        tsum, rs, den, wt = (sb(n, [P, 2, TB]) for n in ("tsum", "rs", "den", "wt"))
        gw = sb("gw", [P, 2, TB, E])
        cum = sb("cum", [E, 2, TB, P], fp16)
        cumL = sb("cumL", [P, NGP, P], fp16)
        cumR = sb("cumR", [P, NGP, M, P], fp16)
        cnt_f = sb("cnt_f", [P, NGP])
        base, nxt = sb("base", [P, NGP]), sb("nxt", [P, NGP])
        jb = sb("jb", [P, NGP, M + 1, 2], fp16)
        ge, oh = sb("ge", [P, CAP], fp16), sb("oh", [P, CAP], fp16)
        ohr = sb("ohr", [P, M, REST], fp16)
        thr, cnt, tok, hit = (sb(n, [P, M + 1]) for n in ("thr", "cnt", "tok", "hit"))
        le = sb("le", [P, M + 1, P], fp16)
        nar = sb("nar", [P, P + 2 * (M + 1)])
        v_all = sb("v_all", [P, NGP, M + 1])
        idx_g, idx_s = sb("idx_g", [P, 2, M + 1], i32), sb("idx_s", [P, 2, M + 1], i32)
        gath = sb("gath", [P, 2, M + 1, ROW])
        ew = [sb(f"ew{m}", [P, 9 * P]) for m in range(M)]
        xe = sb("xe", [P, 2, M, CAP])
        si, ac = sb("si", [P, 2, FC, CAP]), sb("ac", [P, 2, FC, CAP])
        wr_t, wrest = sb("wr_t", [P, M]), sb("wrest", [P, 2])
        ys = sb("ys", [P, M + 2, D])
        vrep, eq, dup_t = sb("vrep", [P, P]), sb("eq", [P, 2, P]), sb("dup_t", [P, P])
        dup, first_, vr = sb("dup", [P, 1]), sb("first", [P, 1]), sb("vr", [P, 1])
        u1, eu, f = (sb(n, [P, TB, 2 * D]) for n in ("u1", "eu", "f"))
        vT = sb("vT", [P, L])
        S_s, qk = sb("S_s", [P, D]), sb("qk", [P, TB, D])
        qks, rq = sb("qks", [P, TB, H]), sb("rq", [P, TB, H])
        o_s, oT_s, y = sb("o_s", [P, TB, D]), sb("oT_s", [P, L]), sb("y", [P, TB, D])
        st2, m2 = sb("st2", [P, TB, 6]), sb("m2", [P, 6, TB])
        yg = sb("yg", [P, TB, D])

        bank = [ctx.enter_context(nc.psum_tensor(f"bank{i}", [P, 512], fp32)) for i in range(8)]

        (s_const, s_w, s_x0, s_x1, s_x2, s_x3) = (sem(n) for n in
            ("const_in", "attw_in", "x_in0", "x_in1", "x_in2", "x_in3"))
        x_in = [s_x0, s_x1, s_x2, s_x3]
        sh_h2, sh_h, sh_si, sh_ac, sh_y = (sem(n) for n in
            ("shared_h2", "shared_h1", "shared_silu", "shared_act", "shared_y"))
        res_out = sem("res_out")
        cast_done, set_done, half_done = sem("cast_done"), sem("set_done"), sem("half_done")
        zero_out, zdone = sem("zero_out"), sem("zdone")
        fold_mm, fold_done = sem("fold_mm"), sem("fold_done")
        stat_d, var_ready, rstd_ready = sem("stat_d"), sem("var_ready"), sem("rstd_ready")
        xm_ready, xn_ready, xb_ready = sem("xm_ready"), sem("xn_ready"), sem("xb_ready")
        xn_out = [sem(f"xn_out{s}") for s in range(2)]
        xTp_ready, xT_ready = sem("xTp_ready"), sem("xT_ready")
        logit_ready, nmax_ready, ex_ready = sem("logit_ready"), sem("nmax_ready"), sem("ex_ready")
        top_ready, left_ready, mask_ready = sem("top_ready"), sem("left_ready"), sem("mask_ready")
        gate_c, wt_c, gw_ready, wrest_c = sem("gate_c"), sem("wt_c"), sem("gw_ready"), sem("wrest_c")
        h2_ready = sem("h2_ready")
        waited, waited_sp = sem("waited"), sem("waited_sp")
        gw_out = [sem(f"gw_out{s}") for s in range(2)]
        cump_ready, cum_ready = sem("cump_ready"), sem("cum_ready")
        cum_out = [sem(f"cum_out{s}") for s in range(2)]
        cum_in, tab_zero, cntf_done = sem("cum_in"), sem("tab_zero"), sem("cntf_done")
        base_mm, base_done, jb_done = sem("base_mm"), sem("base_done"), sem("jb_done")
        oh_ready, tab_mm, tab_step, idx_ready = (sem(n) for n in ("oh_ready", "tab_mm", "tab_step", "idx_ready"))
        idxs_c, nar_done, rest_done = sem("idxs_copied"), sem("narrow_copied"), sem("rest_scaled")
        g_in = [sem(f"gathered{m}") for m in range(M + 1)]
        w_in = [sem(f"expert_in{m}") for m in range(M)]
        s_shw = sem("shared_in")
        xeP, xe_done, wrest_done = sem("xe_psum"), sem("xe_done"), sem("wrest_done")
        h_ready, si_ready, ac_ready, y_ready, y_used = (sem(n) for n in
            ("h_ready", "silu_ready", "act_ready", "y_ready", "y_used"))
        ys_ready, s_sc = sem("ys_ready"), [sem(f"scattered{m}") for m in range(M + 1)]
        vrep_ready, vrepT_ready, eq_step, idxs_ready, sum_mm, ysum_ready = (sem(n) for n in
            ("vrep_ready", "vrepT_ready", "eq_step", "idxrest_ready", "sum_mm", "ysum_ready"))
        qk_ready, v_ready, u_ready, eu_ready, f_ready, vT_done = (sem(n) for n in
            ("qk_ready", "v_ready", "u_ready", "eu_ready", "f_ready", "vT_done"))
        S_ready, Ss_done, qks_step, rq_ready, o_ready, o_done = (sem(n) for n in
            ("S_ready", "S_masked", "qks_step", "rq_ready", "o_ready", "o_done"))
        oTp_ready, oT_done, z_ready, z_used = (sem(n) for n in ("oTp_ready", "oT_done", "z_ready", "z_used"))
        y_step, v2_ready, r2_ready, res_step = (sem(n) for n in ("y_step", "var2_ready", "rstd2_ready", "res_step"))
        out_sem = sem("out_done")

        block = ctx.enter_context(nc.Block())

        xr = x.rearrange("b (j p) d -> p (b j) d", p=P)
        xng_x = xng[0:T, 0:D].rearrange("(b j p) d -> b p j d", p=P, j=TB)
        xng_g = xng[0:T, D:ROW].rearrange("(b j p) d -> b p j d", p=P, j=TB)
        cum_st = cum_d.rearrange("e (b j) t -> b e j t", j=TB)
        res_st = out[0:T, :].rearrange("(b j p) d -> b p j d", p=P, j=TB)
        YS, A1, RT, LG, A0 = bank[3], bank[4], bank[5], bank[6], bank[7]
        Y, R, X, A = (bank[3], bank[4]), bank[5], bank[6], bank[7]
        UNITS = M
        NCONST, NATT_IN, NZERO = 9, 17, 7
        ORDER_G = (M, 0, 1, 2, 3)
        def hview(u, which, n):
            return bank[(2 * u + 1 - which) % 3][:, 0:FC * n].rearrange("p (c n) -> p c n", c=FC)

        @block.sync
        def _(sp):
            for c in range(NC_X):
                sp.dma_start(x_sb[:, c * TC:(c + 1) * TC, :], xr[:, c * TC:(c + 1) * TC, :]).then_inc(x_in[c], 16)
            for dst, src in ((ident, ident_d), (upper_f, upper_d), (before_f, before_d), (slot_f, slot_d),
                             (cols, cols_d), (block4, block4_d), (jrow, jrow_d), (earlier, earlier_d),
                             (head, head_d)):
                sp.dma_start(dst[:, :], src).then_inc(s_const, 16)
            for dst, src in ((wqT_s[:, :], wqT), (wkT_s[:, :], wkT), (wvT_s[:, :], wvT),
                             (w2_s[:, 0, :], wq2), (w2_s[:, 1, :], wk2), (w2_s[:, 2, :], wv2),
                             (wo_s[:, :], wo), (wg_s[:, :], wgT),
                             (bcol[:, 0:1], bq.rearrange("(p a) -> p a", a=1)),
                             (bcol[:, 1:2], bk.rearrange("(p a) -> p a", a=1)),
                             (bcol[:, 2:3], bv.rearrange("(p a) -> p a", a=1)),
                             (bcol[:, 3:4], bv2.rearrange("(p a) -> p a", a=1)),
                             (brow[:, 0, :], bq2.partition_broadcast(P)),
                             (brow[:, 1, :], bk2.partition_broadcast(P)),
                             (bo_b[:, :], bo.partition_broadcast(P)),
                             (gamma_b[:, :], gamma.partition_broadcast(P)),
                             (beta_b[:, :], beta.partition_broadcast(P))):
                sp.dma_start(dst, src).then_inc(s_w, 16)
            sp.dma_start(shw[:, :], shared_w).then_inc(s_shw, 16)
            for m in range(M):
                sp.dma_start(ew[m][:, :], expert_w[m, :, :]).then_inc(w_in[m], 16)

            def step(i, s, residual):
                b = 2 * i + s
                sp.wait_ge(xn_ready, b + 1)
                sp.sem_inc(waited_sp, 1)
                sp.dma_start(xng_x[b, :, :, :], xn[:, s, :, :]).then_inc(xn_out[s], 16)
                if residual:
                    store_residual(b - 2)
                sp.wait_ge(gw_ready, b + 1)
                sp.sem_inc(waited_sp, 1)
                sp.dma_start(xng_g[b, :, :, :], gw[:, s, :, :]).then_inc(gw_out[s], 16)
                sp.wait_ge(cum_ready, b + 1)
                sp.sem_inc(waited_sp, 1)
                sp.dma_start(cum_st[b, :, :, :], cum[:, s, :, :]).then_inc(cum_out[s], 16)

            def store_residual(a):
                sp.wait_ge(res_step, 5 * a + 5)
                sp.sem_inc(waited_sp, 1)
                sp.dma_start(res_st[a, :, :, :], x_sb[:, bass.ds(TB * a, TB), :]).then_inc(res_out, 16)

            step(0, 0, False)
            step(0, 1, False)
            with sp.Fori(1, B // 2) as i:
                step(i, 0, True)
                step(i, 1, True)
            for s in range(2):
                sp.wait_ge(cum_out[s], 16 * B // 2)
            sp.wait_ge(tab_zero, 2)
            for m in range(M):
                src = cum_d.rearrange("(q m) j t -> m j q t", m=M)[m, :, :, :]
                sp.dma_start(cumL[32 * m:32 * m + 32, 0:NG, :], src).then_inc(cum_in, 16)
                sp.dma_start(cumR[32 * m:32 * m + 32, 0:NG, m, :], src).then_inc(cum_in, 16)
            store_residual(B - 2)
            store_residual(B - 1)

            def loads(g):
                for m in range(M):
                    sp.wait_ge(y_ready, UNITS * g + 1 + m)
                    sp.sem_inc(waited_sp, 1)
                    sp.dma_start(ew[m][:, :], expert_w[M * g + M + m, :, :]).then_inc(w_in[m], 16)

            loads(0)
            with sp.Fori(1, NG - 1) as g:
                loads(g)

        @block.gpsimd
        def _(pool):
            pool.memset(half[:, :], -0.5).then_inc(half_done, 1)
            for c in range(NC_X):
                n = slice(c * TC, (c + 1) * TC)
                pool.wait_ge(half_done, 1)
                pool.wait_ge(var_ready, c + 1)
                pool.tensor_tensor(rstd[:, n], var[:, n], half[:, 0:TC], ALU.pow).then_inc(rstd_ready, 1)
            pool.wait_ge(rstd_ready, NC_X)
            pool.wait_ge(s_w, 16 * NATT_IN)
            def normalise(b, i, s):
                tiles = bass.ds(TB * b, TB)
                wide = [P, TB, D]
                xb = x_sb[:, tiles, :]
                pool.tensor_tensor(xm[:, :, :], xb, mean[:, tiles].unsqueeze(2).to_broadcast(wide), ALU.subtract).then_inc(xm_ready, 1)
                pool.wait_ge(xm_ready, b + 1)
                pool.wait_ge(xn_out[s], 16 * i)
                pool.wait_ge(xTp_ready, since(b - 1))
                pool.tensor_tensor(xn[:, s, :, :], xm[:, :, :], rstd[:, tiles].unsqueeze(2).to_broadcast(wide), ALU.mult).then_inc(xn_ready, 1)
                pool.tensor_tensor(xb, xb, beta_b[:, :].unsqueeze(1).to_broadcast(wide), ALU.add).then_inc(xb_ready, 1)
                pool.wait_ge(xn_ready, b + 1)
                pool.tensor_tensor(xnb[:, tiles, :], xn[:, s, :, :], bo_b[:, :].unsqueeze(1).to_broadcast(wide), ALU.add).then_inc(xb_ready, 1)

            def attention_rstd(a):
                pool.wait_ge(v2_ready, a + 1)
                pool.tensor_tensor(m2[:, 5, :], m2[:, 4, :], half[:, 0:TB], ALU.pow).then_inc(r2_ready, 1)

            normalise(0, 0, 0)
            normalise(1, 0, 1)
            normalise(2, 1, 0)
            attention_rstd(0)
            with pool.Fori(1, B // 2 - 1) as i:
                normalise(2 * i + 1, i, 1)
                attention_rstd(2 * i - 1)
                normalise(2 * i + 2, i + 1, 0)
                attention_rstd(2 * i)
            normalise(B - 1, B // 2 - 1, 1)
            pool.memset(cumL[:, :, :], 0.0).then_inc(tab_zero, 1)
            pool.memset(cumR[:, :, :, :], 0.0).then_inc(tab_zero, 1)
            for a in range(B - 3, B):
                attention_rstd(a)
            for s in range(2):
                pool.wait_ge(xn_out[s], 16 * B // 2)
                pool.wait_ge(gw_out[s], 16 * B // 2)
            pool.wait_ge(zero_out, 16 * NZERO)
            added_to = (out, acc)

            def gather(g, p, m):
                if isinstance(g, int) and g == 0:
                    pool.wait_ge(idx_ready, 1)
                else:
                    pool.wait_ge(idx_ready, g + 1)
                    pool.wait_ge(xeP, (M + 1) * (g - 1) + (2 if m in (0, M) else m + 2))
                    pool.sem_inc(waited, 1)
                pool.indirect_dma_start(out=gath[:, p, m, :], out_offset=None, in_=xng,
                                        in_offset=bass.IndirectOffsetOnAxis(ap=idx_g[:, p, m:m + 1], axis=0)
                                        ).then_inc(g_in[m], 16)

            def scatter(g, p, m):
                prev = {0: 3, 1: M, 2: 0, 3: 1, M: 2}[m]
                pool.wait_ge(s_sc[prev], 16 * (g + (1 if m >= 2 else 0)))
                if m < M:
                    pool.wait_ge(idxs_c, g + 1)
                    pool.wait_ge(ys_ready, M * g + m + 1)
                    src = ys[:, m, :]
                else:
                    pool.wait_ge(idxs_ready, g + 1)
                    pool.wait_ge(ysum_ready, g + 1)
                    src = ys[:, M + 1, :]
                pool.sem_inc(waited, 1)
                pool.indirect_dma_start(out=added_to[(p + m) % 2],
                                        out_offset=bass.IndirectOffsetOnAxis(ap=idx_s[:, p, m:m + 1], axis=0),
                                        in_=src, in_offset=None, compute_op=ALU.add).then_inc(s_sc[m], 16)

            def group(g, p, first, last):
                if not first:
                    scatter(g - 1, 1 - p, 2)
                if not last:
                    pool.wait_ge(wrest_done, g)
                    gather(g + 1, 1 - p, M)
                    gather(g + 1, 1 - p, 0)
                if not first:
                    scatter(g - 1, 1 - p, 3)
                if not last:
                    gather(g + 1, 1 - p, 1)
                if not first:
                    scatter(g - 1, 1 - p, M)
                if not last:
                    gather(g + 1, 1 - p, 2)
                scatter(g, p, 0)
                if not last:
                    gather(g + 1, 1 - p, 3)
                scatter(g, p, 1)

            for m in ORDER_G:
                gather(0, 0, m)
            pool.wait_ge(res_out, 16 * B)
            group(0, 0, True, False)
            with pool.Fori(0, NG // 2 - 1) as i:
                group(2 * i + 1, 1, False, False)
                group(2 * i + 2, 0, False, False)
            group(NG - 1, 1, False, True)
            for m in (2, 3, M):
                scatter(NG - 1, 1, m)

            for m in range(M + 1):
                pool.wait_ge(s_sc[m], 16 * NG)
            pool.dma_start(out[0:T, :].rearrange("(p r) d -> p (r d)", p=P), acc[0:T, :].rearrange("(p r) d -> p (r d)", p=P),
                           max_dma_last_dim=4096, accum_op=ALU.add).then_inc(out_sem, 16)
            pool.wait_ge(out_sem, 16)

        @block.scalar
        def _(act):
            act.wait_ge(zdone, 1)
            flat = acc.rearrange("(p r) d -> p (r d)", p=P)
            for k in range(0, flat.shape[1], 1024):
                n = min(1024, flat.shape[1] - k)
                act.dma_start(flat[:, k:k + n], zeros[:, 0:n]).then_inc(zero_out, 16)
            act.dma_start(out[T:T + P, :], zeros[:, 0:D]).then_inc(zero_out, 16)
            act.dma_start(xng[T:T + P, :], zeros[:, 0:ROW]).then_inc(zero_out, 16)
            def shared_silu(a, k):
                act.wait_ge(sh_h2, 2 * a + k + 1)
                act.activation(si[:, k, :, 0:P], hview(k, 1, P), ACT.Silu).then_inc(sh_si, 1)

            def step(b, s, attend):
                a = None if not attend else b - 1 if b is not None else B - 1
                if b is not None:
                    act.wait_ge(xTp_ready, b + 1)
                    act.activation(xT[:, s, :], RT[:, 0:L], ACT.Copy).then_inc(xT_ready, 1)
                if attend:
                    act.wait_ge(u_ready, a + 1)
                    act.wait_ge(f_ready, a)
                    act.activation(eu[:, :, :], u1[:, :, :], ACT.Exp, bias=cols[:, 7:8]).then_inc(eu_ready, 1)
                if b is not None:
                    act.wait_ge(nmax_ready, b + 1)
                    act.wait_ge(gw_ready, since(b - 1))
                    for j in range(TB):
                        act.activation(ex[:, s, j, :], LG[:, j * E:(j + 1) * E], ACT.Exp,
                                       bias=nmax[:, s, j:j + 1], accum_out=esum[:, s, j:j + 1]).then_inc(ex_ready, 1)
                if attend:
                    act.wait_ge(v_ready, a + 1)
                    act.wait_ge(o_ready, a)
                    act.activation(vT[:, :], A1[:, 0:L], ACT.Identity, bias=bvc[:, 0:1]).then_inc(vT_done, 1)
                    shared_silu(a, 0)
                    shared_silu(a, 1)
                if b is not None:
                    act.wait_ge(cump_ready, b + 1)
                    act.wait_ge(cum_out[s], 16 * ((b - s) // 2 if isinstance(b, int) else ring_i))
                    act.activation(cum[:, s, :, :], RT[0:E, 0:L].rearrange("e (j t) -> e j t", j=TB),
                                   ACT.Copy).then_inc(cum_ready, 1)
                if attend:
                    act.wait_ge(oTp_ready, a + 1)
                    act.wait_ge(z_ready, a)
                    act.activation(oT_s[:, :], A1[:, 0:L], ACT.Copy).then_inc(oT_done, 1)

            step(0, 0, False)
            step(1, 1, True)
            with act.Fori(1, B // 2) as ring_i:
                step(2 * ring_i, 0, True)
                step(2 * ring_i + 1, 1, True)
            step(None, 0, True)

            def silu(g, u):
                act.wait_ge(h2_ready, UNITS * g + u + 1)
                act.activation(si[:, u % 2, :, :], hview(u, 1, CAP), ACT.Silu).then_inc(si_ready, 1)

            def xe_copy(g, p, k):
                if k == 0:
                    act.wait_ge(xeP, (M + 1) * g + 2)
                    act.activation(xe[:, p, :, P:CAP], X[:, 0:P].rearrange("p (m r) -> p m r", m=M),
                                   ACT.Copy).then_inc(xe_done, 1)
                else:
                    act.wait_ge(xeP, (M + 1) * g + k + 1)
                    r = 1 if k == 1 else 0
                    act.activation(xe[:, p, k - 1, 0:P], X[:, r * P:(r + 1) * P], ACT.Copy).then_inc(xe_done, 1)

            def y_copy(g, p, m):
                act.wait_ge(y_ready, UNITS * g + 1 + m)
                act.wait_ge(s_sc[m], 16 * g)
                act.activation(ys[:, m, :], Y[m % 2][:, 0:P], ACT.Copy,
                               scale=gath[:, p, m, bass.ds(D + M * g + m, 1)]).then_inc(ys_ready, 1)

            def narrow_copy(q):
                act.wait_ge(tab_mm, q + 1)
                act.wait_ge(idx_ready, q)
                act.activation(nar[:, :], X[:, 0:P + 2 * (M + 1)], ACT.Copy).then_inc(nar_done, 1)

            def rest_copy(g, p):
                act.wait_ge(wrest_done, g + 1)
                act.wait_ge(y_ready, UNITS * (g + 1))
                act.activation(ys[:, M, :], R[:, 0:P], ACT.Copy, scale=wrest[:, p:p + 1]).then_inc(rest_done, 1)

            def sum_copy(g):
                act.wait_ge(sum_mm, g + 1)
                act.wait_ge(s_sc[M], 16 * g)
                act.activation(ys[:, M + 1, :], A[:, 0:P], ACT.Copy).then_inc(ysum_ready, 1)

            def group(g, p, first, last):
                if not first:
                    y_copy(g - 1, 1 - p, 2)
                silu(g, 0)
                xe_copy(g, p, 2)
                if not first:
                    y_copy(g - 1, 1 - p, 3)
                    rest_copy(g - 1, 1 - p)
                silu(g, 1)
                xe_copy(g, p, 3)
                if not first:
                    sum_copy(g - 1)
                y_copy(g, p, 0)
                silu(g, 2)
                xe_copy(g, p, 4)
                y_copy(g, p, 1)
                if not last:
                    narrow_copy(g + 2)
                silu(g, 3)
                if not last:
                    xe_copy(g + 1, 1 - p, 0)
                    xe_copy(g + 1, 1 - p, 1)

            narrow_copy(0)
            narrow_copy(1)
            xe_copy(0, 0, 0)
            xe_copy(0, 0, 1)
            group(0, 0, True, False)
            with act.Fori(0, NG // 2 - 1) as i:
                group(2 * i + 1, 1, False, False)
                group(2 * i + 2, 0, False, False)
            group(NG - 1, 1, False, True)
            y_copy(NG - 1, 1, 2)
            y_copy(NG - 1, 1, 3)
            rest_copy(NG - 1, 1)
            sum_copy(NG - 1)

        @block.vector
        def _(dve):
            dve.memset(ones[:, :], 1.0).then_inc(set_done, 1)
            dve.memset(zeros[:, :], 0.0).then_inc(zdone, 1)
            for c in range(NC_X):
                n = slice(c * TC, (c + 1) * TC)
                dve.wait_ge(x_in[c], 16)
                with dve.Fori(0, TC) as t:
                    dve.bn_stats(st[:, t + c * TC, :], x_sb[:, t + c * TC, :]).then_inc(stat_d, 1)
                k = TC * (c + 1) + 6 * c
                dve.wait_ge(stat_d, k)
                moments(dve, st[:, n, :], m_t, mean[:, n], var[:, n], stat_d, k, EPS_LN, var_ready)
            dve.wait_ge(s_const, 16 * NCONST)
            dve.tensor_copy(upper[:, :], upper_f[:, :]).then_inc(cast_done, 1)
            dve.tensor_copy(before[:, :], before_f[:, :]).then_inc(cast_done, 1)
            dve.tensor_copy(slot[:, :], slot_f[:, :]).then_inc(cast_done, 1)
            dve.wait_ge(s_w, 16 * NATT_IN)
            dve.wait_ge(set_done, 1)
            for k in range(2):
                dve.tensor_scalar(brep[:, k, :], ones[:, :], bcol[:, k:k + 1], None, ALU.mult).then_inc(cast_done, 1)
            dve.wait_ge(fold_mm, 1)
            dve.tensor_copy(wqk[:, :], bank[6][:, 0:2 * D]).then_inc(fold_done, 1)
            dve.tensor_copy(wv[:, :], bank[6][:, 2 * D:3 * D]).then_inc(fold_done, 1)
            dve.scalar_tensor_tensor(bqk1[:, :], bank[7][:, 0:2 * D], 1.0, brow[:, :, :].rearrange("p a n -> p (a n)"),
                                     ALU.add, ALU.add).then_inc(fold_done, 1)
            dve.tensor_tensor(bvc[:, :], bank[7][:, 2 * D:2 * D + 1], bcol[:, 3:4], ALU.add).then_inc(fold_done, 1)
            def shared_act(a, k):
                dve.wait_ge(sh_si, 2 * a + k + 1)
                dve.wait_ge(sh_h, 2 * a + k + 1)
                dve.wait_ge(sh_y, 2 * a)
                dve.tensor_tensor(ac[:, k, :, 0:P], si[:, k, :, 0:P], hview(k, 0, P), ALU.mult).then_inc(sh_ac, 1)

            def finish_scale(a):
                dve.wait_ge(v2_ready, a + 1)
                for j in range(TB):
                    dve.scalar_tensor_tensor(yg[:, j, :], y[:, j, :], m2[:, 3, j:j + 1], gamma_b[:, :], ALU.subtract, ALU.mult).then_inc(res_step, 1)

            def finish_rstd(a):
                dve.wait_ge(res_step, 5 * a + 2)
                dve.wait_ge(r2_ready, a + 1)
                for j in range(TB):
                    dve.tensor_scalar(yg[:, j, :], yg[:, j, :], m2[:, 5, j:j + 1], None, ALU.mult).then_inc(res_step, 1)

            def finish_add(a):
                xg = x_sb[:, bass.ds(TB * a, TB), :]
                dve.wait_ge(res_step, 5 * a + 4)
                dve.wait_ge(y_used, a + 1)
                dve.tensor_tensor(xg, xg, yg[:, :, :], ALU.add).then_inc(res_step, 1)

            def step(b, s, attend, finish):
                route = b is not None
                a = None if not attend else b - 1 if route else B - 1
                if attend:
                    dve.wait_ge(qk_ready, a + 1)
                    dve.wait_ge(eu_ready, a)
                    dve.tensor_tensor(u1[:, :, :], A0[:, :].rearrange("p (j n) -> p j n", j=TB),
                                      bqk1[:, :].unsqueeze(1).to_broadcast([P, TB, 2 * D]), ALU.add).then_inc(u_ready, 1)
                if finish:
                    finish_scale(a - 1)
                if route:
                    dve.wait_ge(logit_ready, b + 1)
                    dve.wait_ge(ex_ready, since(2 * b - 2))
                    dve.tensor_reduce(nmax[:, s, :], LG[:, 0:TB * E].rearrange("p (j e) -> p j e", j=TB),
                                      AX.X, ALU.max, negate=True).then_inc(nmax_ready, 1)
                if finish:
                    finish_rstd(a - 1)
                if attend:
                    dve.wait_ge(eu_ready, a + 1)
                    dve.wait_ge(S_ready, a)
                    dve.scalar_tensor_tensor(f[:, :, :].rearrange("p j n -> p (j n)"), eu[:, :, :].rearrange("p j n -> p (j n)"), 1.0,
                                             u1[:, :, :].rearrange("p j n -> p (j n)"), ALU.min, ALU.max).then_inc(f_ready, 1)
                if finish:
                    finish_add(a - 1)
                if route:
                    dve.wait_ge(ex_ready, 2 * b + 2)
                    dve.reciprocal(rs[:, s, :], esum[:, s, :]).then_inc(gate_c, 1)
                    for j in range(TB):
                        dve.max(top[:, s, j, :], ex[:, s, j, :]).then_inc(top_ready, 1)
                if attend:
                    dve.wait_ge(f_ready, a + 1)
                    dve.tensor_tensor(qk[:, :, :], f[:, :, 0:D], f[:, :, D:2 * D], ALU.mult).then_inc(qks_step, 1)
                    dve.wait_ge(S_ready, a + 1)
                    dve.wait_ge(o_ready, a)
                    dve.tensor_tensor(S_s[:, :], A1[:, 0:P], head[:, :], ALU.mult).then_inc(Ss_done, 1)
                    shared_act(a, 0)
                if route:
                    dve.wait_ge(top_ready, 2 * b + 2)
                    dve.tensor_reduce(tsum[:, s, :], top[:, s, :, :], AX.X, ALU.add).then_inc(gate_c, 1)
                    for j in range(TB):
                        dve.match_replace(left[:, s, j, :], top[:, s, j, :], ex[:, s, j, :], -1.0).then_inc(left_ready, 1)
                if attend:
                    dve.wait_ge(qks_step, 3 * a + 1)
                    dve.tensor_reduce(qks[:, :, :], qk[:, :, :].rearrange("p j (h d) -> p j h d", h=H), AX.X, ALU.add).then_inc(qks_step, 1)
                if route:
                    dve.wait_ge(left_ready, 2 * b + 2)
                    dve.wait_ge(cump_ready, since(b - 1))
                    dve.tensor_scalar(mask[:, s, :, :], left[:, s, :, :], 0.0, None, ALU.is_lt).then_inc(mask_ready, 1)
                if attend:
                    dve.wait_ge(qks_step, 3 * a + 2)
                    dve.tensor_scalar(qks[:, :, :], qks[:, :, :], EPS_QK, None, ALU.add).then_inc(qks_step, 1)
                if route:
                    dve.wait_ge(gate_c, 4 * b + 2)
                    dve.tensor_tensor(den[:, s, :], tsum[:, s, :], rs[:, s, :], ALU.mult).then_inc(gate_c, 1)
                if attend:
                    dve.wait_ge(qks_step, 3 * a + 3)
                    dve.reciprocal(rq[:, :, :], qks[:, :, :]).then_inc(rq_ready, 1)
                if route:
                    dve.wait_ge(gate_c, 4 * b + 3)
                    dve.tensor_scalar(den[:, s, :], den[:, s, :], F32_EPS, None, ALU.max).then_inc(gate_c, 1)
                if attend:
                    dve.wait_ge(o_ready, a + 1)
                    dve.wait_ge(rq_ready, a + 1)
                    dve.wait_ge(oTp_ready, a)
                    dve.tensor_tensor(o_s[:, :, :].rearrange("p j (h d) -> p (j h) d", h=H),
                                      A0[:, 0:TB * D].rearrange("p (n d) -> p n d", d=DH),
                                      rq[:, :, :].rearrange("p j h -> p (j h)").unsqueeze(2).to_broadcast([P, TB * H, DH]),
                                      ALU.mult).then_inc(o_done, 1)
                    shared_act(a, 1)
                if route:
                    dve.wait_ge(gate_c, 4 * b + 4)
                    dve.reciprocal(wt[:, s, :], den[:, s, :]).then_inc(wt_c, 1)
                    dve.wait_ge(wt_c, 2 * b + 1)
                    dve.tensor_tensor(wt[:, s, :], wt[:, s, :], rs[:, s, :], ALU.mult).then_inc(wt_c, 1)
                    dve.wait_ge(wt_c, 2 * b + 2)
                    dve.wait_ge(gw_out[s], 16 * ((b - s) // 2 if isinstance(b, int) else ring_i))
                    dve.tensor_tensor(gw[:, s, :, :], ex[:, s, :, :], wt[:, s, :].unsqueeze(2).to_broadcast([P, TB, E]),
                                      ALU.mult).then_inc(gw_ready, 1)
                if attend:
                    tiles = bass.ds(TB * a, TB)
                    dve.wait_ge(z_ready, a + 1)
                    dve.wait_ge(xb_ready, 2 * a + 2)
                    dve.tensor_tensor(y[:, :, :], A0[:, 0:TB * D].rearrange("p (j n) -> p j n", j=TB), xnb[:, tiles, :], ALU.add).then_inc(z_used, 1)
                    dve.wait_ge(sh_y, 2 * a + 2)
                    dve.tensor_tensor(x_sb[:, tiles, :], x_sb[:, tiles, :], YS[:, 0:TB * D].rearrange("p (j n) -> p j n", j=TB), ALU.add).then_inc(y_used, 1)
                    dve.wait_ge(z_used, a + 1)
                    for j in range(TB):
                        dve.bn_stats(st2[:, j, :], y[:, j, :]).then_inc(y_step, 1)
                    dve.wait_ge(y_step, 8 * a + 2)
                    moments(dve, st2[:, :, :], m2, m2[:, 3, :], m2[:, 4, :], y_step, 8 * a + 2, EPS_ATT, v2_ready)

            step(0, 0, False, False)
            step(1, 1, True, False)
            with dve.Fori(1, B // 2) as ring_i:
                step(2 * ring_i, 0, True, True)
                step(2 * ring_i + 1, 1, True, True)
            step(None, 0, True, True)
            finish_scale(B - 1)
            finish_rstd(B - 1)
            finish_add(B - 1)
            dve.wait_ge(cum_in, 16 * 2 * M)
            dve.tensor_copy(cnt_f[:, :], cumL[:, :, P - 1]).then_inc(cntf_done, 1)
            dve.wait_ge(base_mm, 1)
            dve.tensor_copy(base[:, :], bank[5][:, 0:NGP]).then_inc(base_done, 1)
            dve.wait_ge(cntf_done, 1)
            dve.tensor_tensor(nxt[:, :], bank[5][:, 0:NGP], cnt_f[:, :], ALU.add).then_inc(base_done, 1)
            dve.wait_ge(base_done, 2)
            for m in range(M):
                dve.tensor_scalar(jb[:, :, m, 1], base[:, :], block4[:, m:m + 1], None, ALU.mult).then_inc(jb_done, 1)
            dve.tensor_copy(jb[:, :, M, 1], base[:, :]).then_inc(jb_done, 1)
            dve.tensor_copy(jb[:, :, :, 0], jrow[:, :].unsqueeze(1).to_broadcast([P, NGP, M + 1])).then_inc(jb_done, 1)

            def table_hot(q):
                dve.wait_ge(tab_mm, q)
                dve.tensor_scalar(ge[:, :], slot[:, :], base[:, bass.ds(q, 1)], None, ALU.is_ge).then_inc(oh_ready, 1)
                dve.wait_ge(oh_ready, 3 * q + 1)
                dve.scalar_tensor_tensor(oh[:, :], slot[:, :], nxt[:, bass.ds(q, 1)], ge[:, :], ALU.is_lt, ALU.mult).then_inc(oh_ready, 1)
                dve.wait_ge(oh_ready, 3 * q + 2)
                dve.tensor_tensor(ohr[:, :, :], oh[:, P:CAP].unsqueeze(1).to_broadcast([P, M, REST]),
                                  block4[:, :].unsqueeze(2).to_broadcast([P, M, REST]), ALU.mult).then_inc(oh_ready, 1)

            small = nar[:, P:P + 2 * (M + 1)].rearrange("p (k a) -> p k a", a=2)
            N = 8

            def table_compare(q):
                dve.wait_ge(nar_done, q + 1)
                dve.tensor_tensor(thr[:, :], cols[:, 0:M + 1], small[:, :, 1], ALU.subtract).then_inc(tab_step, 1)
                dve.wait_ge(tab_step, N * q + 1)
                dve.tensor_tensor(le[:, 0:M, :], A[:, :].rearrange("p (m t) -> p m t", m=M),
                                  thr[:, 0:M].unsqueeze(2).to_broadcast([P, M, P]), ALU.is_le).then_inc(tab_step, 1)
                dve.tensor_scalar(le[:, M, :], nar[:, 0:P], thr[:, M:M + 1], None, ALU.is_le).then_inc(tab_step, 1)
                dve.tensor_scalar(hit[:, :], small[:, :, 0], 0.0, None, ALU.is_gt).then_inc(tab_step, 1)

            def table_tokens(q, p):
                dve.wait_ge(tab_step, N * q + 4)
                dve.tensor_reduce(cnt[:, :], le[:, :, :], AX.X, ALU.add).then_inc(tab_step, 1)
                dve.wait_ge(tab_step, N * q + 5)
                dve.scalar_tensor_tensor(tok[:, :], small[:, :, 0], float(P), cnt[:, :], ALU.mult, ALU.add).then_inc(tab_step, 1)
                dve.wait_ge(tab_step, N * q + 6)
                dve.scalar_tensor_tensor(tok[:, :], tok[:, :], cols[:, 6:7], hit[:, :], ALU.subtract, ALU.mult).then_inc(tab_step, 1)
                dve.wait_ge(tab_step, N * q + 7)
                dve.tensor_scalar(v_all[:, q, :], tok[:, :], cols[:, 5:6], None, ALU.add).then_inc(tab_step, 1)
                dve.tensor_scalar(idx_g[:, p, :], tok[:, :], cols[:, 5:6], None, ALU.add).then_inc(idx_ready, 1)

            def act_mul(g, u):
                dve.wait_ge(si_ready, UNITS * g + u + 1)
                dve.wait_ge(h_ready, UNITS * g + u + 1)
                dve.wait_ge(y_ready, since(UNITS * g + u - 1))
                dve.tensor_tensor(ac[:, u % 2, :, :], si[:, u % 2, :, :], hview(u, 0, CAP), ALU.mult).then_inc(ac_ready, 1)

            def group(g, p, first, last):
                vM = v_all[:, g, M:M + 1]
                dve.wait_ge(idx_ready, g + 1)
                if not first:
                    act_mul(g - 1, 3)
                if not last:
                    table_tokens(g + 1, 1 - p)
                dve.wait_ge(vrepT_ready, g)
                dve.tensor_scalar(vrep[:, :], ones[:, :], vM, None, ALU.mult).then_inc(vrep_ready, 1)
                dve.wait_ge(vrepT_ready, g + 1)
                dve.wait_ge(sum_mm, since(g - 1))
                dve.tensor_scalar(eq[:, p, :], A[:, 0:P], vM, None, ALU.is_equal).then_inc(eq_step, 1)
                act_mul(g, 0)
                if not first:
                    dve.wait_ge(s_sc[3], 16 * (g - 1))
                    dve.wait_ge(s_sc[M], 16 * (g - 1))
                dve.tensor_copy(idx_s[:, p, 0:M], idx_g[:, p, 0:M]).then_inc(idxs_c, 1)
                dve.tensor_tensor(wr_t[:, :], gath[:, p, M, bass.ds(D + M * g, M)], block4[:, :], ALU.mult).then_inc(wrest_c, 1)
                dve.wait_ge(wrest_c, g + 1)
                dve.wait_ge(rest_done, since(g - 1))
                dve.tensor_reduce(wrest[:, p:p + 1], wr_t[:, :], AX.X, ALU.add).then_inc(wrest_done, 1)
                if not last:
                    table_hot(g + 2)
                act_mul(g, 1)
                dve.wait_ge(eq_step, 5 * g + 1)
                dve.tensor_tensor(dup_t[:, :], eq[:, p, :], earlier[:, :], ALU.mult).then_inc(eq_step, 1)
                dve.wait_ge(eq_step, 5 * g + 2)
                dve.tensor_reduce(dup[:, :], dup_t[:, :], AX.X, ALU.add).then_inc(eq_step, 1)
                dve.wait_ge(eq_step, 5 * g + 3)
                dve.tensor_scalar(first_[:, :], dup[:, :], 0.5, None, ALU.is_lt).then_inc(eq_step, 1)
                dve.wait_ge(eq_step, 5 * g + 4)
                dve.scalar_tensor_tensor(vr[:, :], vM, cols[:, 5:6], first_[:, :], ALU.subtract, ALU.mult).then_inc(eq_step, 1)
                dve.wait_ge(eq_step, 5 * g + 5)
                dve.tensor_scalar(idx_s[:, p, M:M + 1], vr[:, :], cols[:, 5:6], None, ALU.add).then_inc(idxs_ready, 1)
                act_mul(g, 2)
                if not last:
                    table_compare(g + 2)

            table_hot(0)
            dve.wait_ge(jb_done, M + 2)
            table_compare(0)
            table_tokens(0, 0)
            table_hot(1)
            table_compare(1)
            group(0, 0, True, False)
            with dve.Fori(0, NG // 2 - 1) as i:
                group(2 * i + 1, 1, False, False)
                group(2 * i + 2, 0, False, False)
            group(NG - 1, 1, False, True)
            act_mul(NG - 1, 3)

        @block.tensor
        def _(pe):
            pe.wait_ge(s_w, 16 * NATT_IN)
            pe.matmul(bank[6][:, 0:D], wqT_s[:, :], w2_s[:, 0, :], start=True, stop=True)
            pe.matmul(bank[6][:, D:2 * D], wkT_s[:, :], w2_s[:, 1, :], start=True, stop=True)
            pe.matmul(bank[6][:, 2 * D:3 * D], wvT_s[:, :], w2_s[:, 2, :], start=True, stop=True)
            pe.wait_ge(cast_done, 5)
            for k in range(2):
                pe.matmul(bank[7][:, k * D:(k + 1) * D], brep[:, k, :], w2_s[:, k, :], start=True, stop=True)
            pe.matmul(bank[7][:, 2 * D:2 * D + 1], w2_s[:, 2, :], bcol[:, 2:3], start=True, stop=True).then_inc(fold_mm, 1)
            def shared_up(a, k, sa):
                for half_ in (1, 0):
                    pe.wait_ge(sh_ac, 2 * a)
                    pe.wait_ge(sh_si, 2 * a + (k if half_ == 0 else 0))
                    for c in range(FC):
                        w = shw[:, (half_ * FC + c) * P:(half_ * FC + c + 1) * P]
                        last = pe.matmul(hview(k, half_, P)[:, c, :], w, xT[:, sa, k * P:(k + 1) * P], start=True, stop=True)
                    last.then_inc(sh_h2 if half_ else sh_h, 1)

            def shared_down(a, k):
                pe.wait_ge(sh_ac, 2 * a + k + 1)
                pe.wait_ge(y_used, a)
                for c in range(FC):
                    last = pe.matmul(YS[:, k * P:(k + 1) * P], ac[:, k, c, 0:P], shw[:, (2 * FC + c) * P:(2 * FC + c + 1) * P],
                                     start=(c == 0), stop=(c == FC - 1))
                last.then_inc(sh_y, 1)

            def step(b, s, attend):
                route = b is not None
                a = None if not attend else b - 1 if route else B - 1
                sa = 1 - s
                if route:
                    pe.wait_ge(xn_ready, b + 1)
                    pe.wait_ge(cum_ready, b)
                    for j in range(TB):
                        last = pe.transpose(RT[:, j * P:(j + 1) * P], xn[:, s, j, :], ident[:, :])
                    last.then_inc(xTp_ready, 1)
                if attend:
                    pe.wait_ge(z_used, a)
                    for j in range(TB):
                        last = pe.matmul(A0[:, j * 2 * D:(j + 1) * 2 * D], xT[:, sa, j * P:(j + 1) * P], wqk[:, :], start=True, stop=True)
                    last.then_inc(qk_ready, 1)
                if route:
                    pe.wait_ge(xT_ready, b + 1)
                    pe.wait_ge(ex_ready, 2 * b)
                    for j in range(TB):
                        last = pe.matmul(LG[:, j * E:(j + 1) * E], xT[:, s, j * P:(j + 1) * P], wg_s[:, :], start=True, stop=True)
                    last.then_inc(logit_ready, 1)
                if attend:
                    pe.wait_ge(oT_done, a)
                    pe.matmul(A1[:, 0:L], wv[:, :], xT[:, sa, :], start=True, stop=True).then_inc(v_ready, 1)
                    shared_up(a, 0, sa)
                    pe.wait_ge(f_ready, a + 1)
                    pe.wait_ge(vT_done, a + 1)
                    for j in range(TB):
                        last = pe.matmul(A1[:, 0:P], f[:, j, D:2 * D], f[:, j, 0:D], start=(j == 0), stop=(j == TB - 1))
                    last.then_inc(S_ready, 1)
                    shared_up(a, 1, sa)
                    pe.wait_ge(Ss_done, a + 1)
                    pe.wait_ge(u_ready, a + 1)
                    for j in range(TB):
                        last = pe.matmul(A0[:, j * D:(j + 1) * D], vT[:, j * P:(j + 1) * P], S_s[:, :], start=True, stop=True)
                    last.then_inc(o_ready, 1)
                    shared_down(a, 0)
                if route:
                    pe.wait_ge(mask_ready, b + 1)
                    for j in range(TB):
                        last = pe.matmul(RT[0:E, j * P:(j + 1) * P], mask[:, s, j, :], upper[:, :], start=True, stop=True)
                    last.then_inc(cump_ready, 1)
                if attend:
                    pe.wait_ge(o_done, a + 1)
                    for j in range(TB):
                        last = pe.transpose(A1[:, j * P:(j + 1) * P], o_s[:, j, :], ident[:, :])
                    last.then_inc(oTp_ready, 1)
                    shared_down(a, 1)
                    pe.wait_ge(oT_done, a + 1)
                    for j in range(TB):
                        last = pe.matmul(A0[:, j * D:(j + 1) * D], oT_s[:, j * P:(j + 1) * P], wo_s[:, :], start=True, stop=True)
                    last.then_inc(z_ready, 1)

            pe.wait_ge(fold_done, 4)
            pe.wait_ge(s_shw, 16)
            step(0, 0, False)
            step(1, 1, True)
            with pe.Fori(1, B // 2) as i:
                step(2 * i, 0, True)
                step(2 * i + 1, 1, True)
            step(None, 0, True)
            pe.wait_ge(cum_in, 16 * 2 * M)
            pe.matmul(bank[5][:, 0:NGP], before[:, :], cumL[:, :, P - 1], start=True, stop=True).then_inc(base_mm, 1)

            def table(q):
                pe.wait_ge(oh_ready, 3 * q + 3)
                pe.matmul(A[:, :], oh[:, 0:P], cumR[:, q, :, :].rearrange("p m t -> p (m t)"), start=True, stop=True)
                pe.matmul(X[:, P:P + 8], oh[:, 0:P], jb[:, q, 0:M, :].rearrange("p m a -> p (m a)"), start=True, stop=True)
                pe.matmul(X[:, 0:P], ohr[:, :, :].rearrange("p m r -> p (m r)"), cumL[:, q, :], start=True, stop=True)
                pe.matmul(X[:, P + 8:P + 10], ohr[:, :, :].rearrange("p m r -> p (m r)"), jb[:, q, M, :], start=True, stop=True).then_inc(tab_mm, 1)

            def up(g, p, u):
                pe.wait_ge(xe_done, (M + 1) * g + u + 2)
                pe.wait_ge(w_in[u], 16 * g + 16)
                for half_ in (1, 0):
                    if u > 0 and half_ == 1:
                        pe.wait_ge(ac_ready, since(UNITS * g + u - 1))
                    else:
                        pe.wait_ge(si_ready, UNITS * g + u)
                        if u == 0 and half_ == 0:
                            pe.wait_ge(ac_ready, UNITS * g)
                    for c in range(FC):
                        k = half_ * FC + c
                        last = pe.matmul(hview(u, half_, CAP)[:, c, :], ew[u][:, k * P:(k + 1) * P], xe[:, p, u, :], start=True, stop=True)
                    last.then_inc(h2_ready if half_ else h_ready, 1)

            def down(g, m):
                r = m % 2
                pe.wait_ge(ac_ready, UNITS * g + m + 1)
                pe.wait_ge(ys_ready, since(M * g + m - 1))
                for c in range(FC):
                    pe.matmul(Y[r][:, 0:P], ac[:, r, c, 0:P], ew[m][:, (6 + c) * P:(7 + c) * P],
                              start=(c == 0), stop=(c == FC - 1))
                if m == 0:
                    pe.wait_ge(rest_done, g)
                for c in range(FC):
                    last = pe.matmul(R[32 * m:32 * m + 32, 0:P], ac[:, r, c, P:CAP], ew[m][:, (6 + c) * P:(7 + c) * P],
                                     start=(c == 0), stop=(c == FC - 1))
                last.then_inc(y_ready, 1)

            def rows_T(g, p, k):
                if k == 1:
                    pe.wait_ge(nar_done, g + 2)
                    pe.wait_ge(g_in[M], 16 * g + 16)
                    pe.transpose(X[:, 0:P], gath[:, p, M, 0:D], ident[:, :])
                    pe.wait_ge(g_in[0], 16 * g + 16)
                    pe.transpose(X[:, P:2 * P], gath[:, p, 0, 0:D], ident[:, :]).then_inc(xeP, 2)
                else:
                    pe.wait_ge(g_in[k - 1], 16 * g + 16)
                    pe.wait_ge(xe_done, (M + 1) * g + k)
                    pe.transpose(X[:, 0:P], gath[:, p, k - 1, 0:D], ident[:, :]).then_inc(xeP, 1)

            def rest_sum(g, p):
                pe.wait_ge(rest_done, g + 1)
                pe.matmul(A[:, 0:P], eq[:, p, :], ys[:, M, :], start=True, stop=True).then_inc(sum_mm, 1)

            def group(g, p, first, last):
                up(g, p, 0)
                rows_T(g, p, 2)
                if not first:
                    down(g - 1, 3)
                pe.wait_ge(vrep_ready, g + 1)
                pe.wait_ge(tab_step, 8 * (g + 1) + 2)
                pe.transpose(A[:, 0:P], vrep[:, :], ident[:, :]).then_inc(vrepT_ready, 1)
                up(g, p, 1)
                rows_T(g, p, 3)
                pe.wait_ge(eq_step, 5 * g + 1)
                if not first:
                    rest_sum(g - 1, 1 - p)
                down(g, 0)
                up(g, p, 2)
                rows_T(g, p, 4)
                down(g, 1)
                if not last:
                    pe.wait_ge(ysum_ready, g)
                    pe.wait_ge(xe_done, (M + 1) * (g + 1))
                    table(g + 2)
                up(g, p, 3)
                if not last:
                    rows_T(g + 1, 1 - p, 1)
                down(g, 2)

            pe.wait_ge(jb_done, M + 2)
            table(0)
            pe.wait_ge(idx_ready, 1)
            table(1)
            rows_T(0, 0, 1)
            group(0, 0, True, False)
            with pe.Fori(0, NG // 2 - 1) as i:
                group(2 * i + 1, 1, False, False)
                group(2 * i + 2, 0, False, False)
            group(NG - 1, 1, False, True)
            down(NG - 1, 3)
            rest_sum(NG - 1, 1)


_VECTORS = ['bq', 'bk', 'bv', 'bq2', 'bk2', 'bv2', 'bo', 'gamma', 'beta']


def kernel(**inputs):
    import numpy as _np
    import concourse.bacc as _bacc
    from concourse import mybir as _mybir
    from concourse.bass_utils import run_bass_kernel_spmd as _run

    a = {n: _np.asarray(v) for n, v in inputs.items()}
    P, M = 128, 4
    x = a['L0_attn_x']
    B, L, D = x.shape
    NT = B * L // P

    def packed(w1, w2):
        up = _np.swapaxes(w1, -1, -2)
        down = _np.swapaxes(w2, -1, -2)
        c = down.shape[-2] // P
        down = down.reshape(down.shape[:-2] + (c, P, D))
        down = _np.swapaxes(down, -3, -2).reshape(down.shape[:-3] + (P, c * D))
        return _np.concatenate([up, down], axis=-1)

    arrays = {'x': x}
    for n in ('Wq', 'Wk', 'Wv'):
        arrays[n + 'T'] = a['L0_attn_' + n].T
    for n in ('Wq2', 'Wk2', 'Wv2', 'Wo'):
        arrays[n] = a['L0_attn_' + n]
    for n in _VECTORS:
        arrays[n] = a['L0_attn_' + n]
    arrays['wgT'] = a['L0_ffn_wg'].T
    arrays['shared_w'] = packed(a['L0_ffn_shared_w1'], a['L0_ffn_shared_w2'])
    arrays['expert_w'] = packed(a['L0_ffn_expert_w1'], a['L0_ffn_expert_w2'])

    p = _np.arange(P)
    row, col = p[:, None], p[None, :]
    rest = P + p % 32
    cols = _np.stack([p, p, p, p, rest, B * L + p, B * L + p + P, -_np.ones(P)], axis=1)
    block4 = (row // 32 == _np.arange(M)[None, :])
    jrow = _np.concatenate([block4 * (row % 32 + 1), row % 32 + 1], axis=1)
    constants = {
        'ident': row == col,
        'upper': row <= col,
        'before': (row // 32 == col // 32) & (row < col),
        'slots': _np.broadcast_to(_np.arange(160)[None, :], (P, 160)),
        'cols': cols,
        'block4': block4,
        'jrow': jrow,
        'earlier': col < row,
        'head': row // 8 == col // 8,
    }
    for n, v in constants.items():
        arrays['c_' + n] = v.astype(_np.float32)

    nc = _bacc.Bacc("TRN2", target_bir_lowering=False, num_devices=1)
    given, args = {}, []
    for n, v in arrays.items():
        v = _np.ascontiguousarray(v)
        given[f"in_{n}"] = v
        args.append(nc.dram_tensor(f"in_{n}", v.shape, _mybir.dt.from_np(v.dtype), kind="ExternalInput").ap())
    args.append(nc.dram_tensor("out_0", (B * L + P, D), _mybir.dt.float32, kind="ExternalOutput").ap())
    block_kernel(nc, *args)
    r = _run(nc, [given], core_ids=[0])
    return r.results[0]["out_0"][:B * L].reshape(B, L, D)
```

```python
import concourse.bass as bass
from concourse import mybir
from contextlib import ExitStack



def since(count):
    return max(count, 0) if isinstance(count, int) else count


def moments(eng, s, t, mean, var, step, k, eps, done, sign=1.0, stages=(0, 1, 2, 3)):
    ALU = mybir.AluOpType
    t0, t1, t2 = t[:, 0, :], t[:, 1, :], t[:, 2, :]
    for stage in stages:
        if stage == 0:
            eng.wait_ge(step, k)
            eng.tensor_tensor(t0, s[:, :, 1], s[:, :, 4], ALU.add).then_inc(step, 1)
            eng.tensor_tensor(t1, s[:, :, 1], s[:, :, 4], ALU.subtract).then_inc(step, 1)
            eng.tensor_tensor(t2, s[:, :, 2], s[:, :, 5], ALU.add).then_inc(step, 1)
        elif stage == 1:
            eng.wait_ge(step, k + 3)
            eng.tensor_scalar(mean, t0, 0.5 * sign, None, ALU.mult).then_inc(step, 1)
            eng.scalar_tensor_tensor(t1, t1, 0.25, t1, ALU.mult, ALU.mult).then_inc(step, 1)
        elif stage == 2:
            eng.wait_ge(step, k + 5)
            eng.scalar_tensor_tensor(t2, t2, 1.0 / 128, t1, ALU.mult, ALU.add).then_inc(step, 1)
        else:
            eng.wait_ge(step, k + 6)
            eng.tensor_scalar(var, t2, eps, None, ALU.add).then_inc(done, 1)


def block_kernel(nc, x, weights_d, vectors_d, shared_w, expert_w, const_d, out):
    fp32, fp16, bf16, i32 = mybir.dt.float32, mybir.dt.float16, mybir.dt.bfloat16, mybir.dt.int32
    ALU, ACT, AX = mybir.AluOpType, mybir.ActivationFunctionType, mybir.AxisListType

    P = 128
    B, L, D = x.shape
    T = B * L
    NT = T // P
    TB = L // P
    E = expert_w.shape[0]
    M = 4
    NG = E // M
    CAP, TOPK = 160, 8
    REST = CAP - P
    FC = expert_w.shape[2] // P // 3
    ROW = D + E
    H, DH = 16, D // 16
    NGP = NG + 1
    EPS_LN, EPS_ATT, EPS_QK = 1e-5, 1e-3, 1e-6
    F32_EPS = 1.1920929e-07
    ENDS = (0, TB, NT // 4, NT // 2, 3 * NT // 4, NT)
    NC_X = len(ENDS) - 1
    assert NG == B and M * NT == P and P + REST == CAP

    ctx = ExitStack()
    with ctx:
        def sb(name, shape, dt=fp32):
            return ctx.enter_context(nc.sbuf_tensor(name, shape, dt))

        def sem(name):
            return ctx.enter_context(nc.semaphore(name))

        def dram(name, shape, dt=fp32):
            return nc.dram_tensor(name, shape, dt, kind="Internal").ap()

        xng = dram("xng", [T + P, ROW])
        cum_d = dram("cum_d", [E, NT, P], fp16)
        acc = dram("acc", [T + P, D])

        cpack = sb("cpack", [P, const_d.shape[1]])
        k = 0

        def const(width):
            nonlocal k
            k += width
            return cpack[:, k - width:k]

        ident, upper_f, before_f = const(P), const(P), const(P)
        earlier, head = const(P), const(P)
        slot_f = const(CAP)
        cols = const(8)
        block4 = const(M)
        jrow = const(M + 1)
        assert k == const_d.shape[1]
        upper = sb("upper", [P, P], bf16)
        before = sb("before", [P, P], fp16)
        slot = sb("slot", [P, CAP], fp16)
        ones, half = sb("ones", [P, P]), sb("half", [P, 8])
        zeros = sb("zeros", [P, 1024])
        wpack = sb("wpack", [P, weights_d.shape[1]])
        wqT_s, wkT_s, wvT_s = (wpack[:, k * D:(k + 1) * D] for k in range(3))
        w2_s = wpack[:, 3 * D:6 * D].rearrange("p (k d) -> p k d", k=3)
        wo_s, wg_s = wpack[:, 6 * D:7 * D], wpack[:, 7 * D:7 * D + E]
        bcol = wpack[:, 7 * D + E:7 * D + E + 4]
        vpack = sb("vpack", [P, vectors_d.shape[0]])
        brow = vpack[:, 0:2 * D].rearrange("p (k d) -> p k d", k=2)
        bo_b, gamma_b, beta_b = (vpack[:, k * D:(k + 1) * D] for k in range(2, 5))
        brep = sb("brep", [P, 2, P])
        wqk = sb("wqk", [P, 2 * D])
        wv = sb("wv", [P, D])
        bqk1 = sb("bqk1", [P, 2 * D])
        bvc = sb("bvc", [P, 1])
        shw = sb("shw", [P, 9 * P])
        x_sb = sb("x_sb", [P, NT, D])
        xnb = sb("xnb", [P, NT, D])
        st = sb("st", [P, NT, 6])
        mean, var, rstd = sb("mean", [P, NT]), sb("var", [P, NT]), sb("rstd", [P, NT])
        m_t = sb("m_t", [P, 4, NT // 4])
        xm = sb("xm", [P, TB, D])
        xn = sb("xn", [P, 2, TB, D])
        xT = sb("xT", [P, 2, L])
        nmax, esum = sb("nmax", [P, 2, TB]), sb("esum", [P, 2, TB])
        ex = sb("ex", [P, 2, TB, E])
        top = sb("top", [P, 2, TB, TOPK])
        left = sb("left", [P, 2, TB, E])
        mask = sb("mask", [P, 2, TB, E], bf16)
        tsum, rs, den, wt = (sb(n, [P, 2, TB]) for n in ("tsum", "rs", "den", "wt"))
        gw = sb("gw", [P, 2, TB, E])
        cum = sb("cum", [E, 2, TB, P], fp16)
        cumL = sb("cumL", [P, NGP, P], fp16)
        cumR = sb("cumR", [P, NGP, M, P], fp16)
        cnt_f = sb("cnt_f", [P, NGP])
        base, nxt = sb("base", [P, NGP]), sb("nxt", [P, NGP])
        jb = sb("jb", [P, NGP, M + 1, 2], fp16)
        ge, oh = sb("ge", [P, CAP], fp16), sb("oh", [P, CAP], fp16)
        ohr = sb("ohr", [P, M, REST], fp16)
        thr, cnt, tok, hit = (sb(n, [P, M + 1]) for n in ("thr", "cnt", "tok", "hit"))
        le = sb("le", [P, M + 1, P], fp16)
        nar = sb("nar", [P, P + 2 * (M + 1)])
        v_all = sb("v_all", [P, NGP, M + 1])
        idx_g, idx_s = sb("idx_g", [P, 2, M + 1], i32), sb("idx_s", [P, 2, M + 1], i32)
        gath = sb("gath", [P, 2, M + 1, ROW])
        ew = [sb(f"ew{m}", [P, 9 * P]) for m in range(M)]
        xe = sb("xe", [P, 2, M, CAP])
        si, ac = sb("si", [P, 2, FC, CAP]), sb("ac", [P, 2, FC, CAP])
        wr_t, wrest = sb("wr_t", [P, M]), sb("wrest", [P, 2])
        ys = sb("ys", [P, M + 2, D])
        vrep, eq, dup_t = sb("vrep", [P, P]), sb("eq", [P, 2, P]), sb("dup_t", [P, P])
        dup, first_, vr = sb("dup", [P, 1]), sb("first", [P, 1]), sb("vr", [P, 1])
        u1, eu, f = (sb(n, [P, TB, 2 * D]) for n in ("u1", "eu", "f"))
        vT = sb("vT", [P, L])
        S_s, qk = sb("S_s", [P, D]), sb("qk", [P, TB, D])
        qks, rq = sb("qks", [P, TB, H]), sb("rq", [P, TB, H])
        o_s, oT_s, y = sb("o_s", [P, TB, D]), sb("oT_s", [P, L]), sb("y", [P, 2, TB, D])
        st2, m2 = sb("st2", [P, TB, 6]), sb("m2", [P, 6, TB])
        yg, nb, scrap = sb("yg", [P, TB, D]), sb("nb", [P, TB]), sb("scrap", [P, 1])

        bank = [ctx.enter_context(nc.psum_tensor(f"bank{i}", [P, 512], fp32)) for i in range(8)]

        (s_const, s_w, s_x0, s_x1, s_x2, s_x3, s_x4) = (sem(n) for n in
            ("const_in", "attw_in", "x_in0", "x_in1", "x_in2", "x_in3", "x_in4"))
        x_in = [s_x0, s_x1, s_x2, s_x3, s_x4]
        sh_h2, sh_h, sh_si, sh_ac, sh_y = (sem(n) for n in
            ("shared_h2", "shared_h1", "shared_silu", "shared_act", "shared_y"))
        res_out = sem("res_out")
        cast_done, set_done, half_done = sem("cast_done"), sem("set_done"), sem("half_done")
        zero_out, zdone = sem("zero_out"), sem("zdone")
        fold_mm, fold_done = sem("fold_mm"), sem("fold_done")
        stat_d, var_ready, rstd_ready = sem("stat_d"), sem("var_ready"), sem("rstd_ready")
        xm_ready, xn_ready, xb_ready = sem("xm_ready"), sem("xn_ready"), sem("xb_ready")
        xn_out = [sem(f"xn_out{s}") for s in range(2)]
        xTp_ready, xT_ready = sem("xTp_ready"), sem("xT_ready")
        logit_ready, nmax_ready, ex_ready = sem("logit_ready"), sem("nmax_ready"), sem("ex_ready")
        top_ready, left_ready, mask_ready = sem("top_ready"), sem("left_ready"), sem("mask_ready")
        gate_c, wt_c, gw_ready, wrest_c = sem("gate_c"), sem("wt_c"), sem("gw_ready"), sem("wrest_c")
        h2_ready = sem("h2_ready")
        waited, waited_sp = sem("waited"), sem("waited_sp")
        gw_out = [sem(f"gw_out{s}") for s in range(2)]
        cump_ready, cum_ready = sem("cump_ready"), sem("cum_ready")
        cum_out = [sem(f"cum_out{s}") for s in range(2)]
        cum_in, tab_zero, cntf_done = sem("cum_in"), sem("tab_zero"), sem("cntf_done")
        base_mm, base_done, jb_done = sem("base_mm"), sem("base_done"), sem("jb_done")
        oh_ready, tab_mm, tab_step, idx_ready = (sem(n) for n in ("oh_ready", "tab_mm", "tab_step", "idx_ready"))
        idxs_c, nar_done, rest_done = sem("idxs_copied"), sem("narrow_copied"), sem("rest_scaled")
        g_in = [sem(f"gathered{m}") for m in range(M + 1)]
        w_in = [sem(f"expert_in{m}") for m in range(M)]
        s_shw = sem("shared_in")
        xeP, xe_done, wrest_done = sem("xe_psum"), sem("xe_done"), sem("wrest_done")
        h_ready, si_ready, ac_ready, y_ready, y_used = (sem(n) for n in
            ("h_ready", "silu_ready", "act_ready", "y_ready", "y_used"))
        ys_ready, s_sc = sem("ys_ready"), [sem(f"scattered{m}") for m in range(M + 1)]
        vrep_ready, vrepT_ready, eq_step, idxs_ready, sum_mm, ysum_ready = (sem(n) for n in
            ("vrep_ready", "vrepT_ready", "eq_step", "idxrest_ready", "sum_mm", "ysum_ready"))
        qk_ready, v_ready, u_ready, eu_ready, f_ready, vT_done = (sem(n) for n in
            ("qk_ready", "v_ready", "u_ready", "eu_ready", "f_ready", "vT_done"))
        S_ready, Ss_done, qks_step, rq_ready, o_ready, o_done = (sem(n) for n in
            ("S_ready", "S_masked", "qks_step", "rq_ready", "o_ready", "o_done"))
        oTp_ready, oT_done, z_ready, z_used = (sem(n) for n in ("oTp_ready", "oT_done", "z_ready", "z_used"))
        y_step, v2_ready, r2_ready, res_done = (sem(n) for n in ("y_step", "var2_ready", "rstd2_ready", "res_done"))
        yn_ready, yg_ready, qk_prod = (sem(n) for n in ("y_normed", "yg_ready", "qk_product"))
        cumL_zero, cumR_in = sem("cumL_zero"), sem("cumR_in")
        out_sem = sem("out_done")

        block = ctx.enter_context(nc.Block())

        xr = x.rearrange("b (j p) d -> p (b j) d", p=P)
        xng_x = xng[0:T, 0:D].rearrange("(b j p) d -> b p j d", p=P, j=TB)
        xng_g = xng[0:T, D:ROW].rearrange("(b j p) d -> b p j d", p=P, j=TB)
        cum_st = cum_d.rearrange("e (b j) t -> b e j t", j=TB)
        res_st = out[0:T, :].rearrange("(b j p) d -> b p j d", p=P, j=TB)
        YS, RT, LG = bank[3], bank[5], bank[6]
        AQ, AV = (bank[7], bank[4]), (bank[4], bank[7])

        def sh_view(k, which):
            t = LG[:, TB * E:TB * E + FC * P] if (k, which) == (1, 0) else bank[2 * k + 1 - which][:, 0:FC * P]
            return t.rearrange("p (c n) -> p c n", c=FC)

        Y, R, X, A = (bank[3], bank[4]), bank[5], bank[6], bank[7]
        UNITS = M
        NZERO = 7
        def hview(u, which, n):
            return bank[(2 * u + 1 - which) % 3][:, 0:FC * n].rearrange("p (c n) -> p c n", c=FC)

        @block.sync
        def _(sp):
            def small_loads():
                sp.dma_start(wpack[:, :], weights_d).then_inc(s_w, 16)
                sp.dma_start(vpack[:, :], vectors_d.partition_broadcast(P)).then_inc(s_w, 16)
                sp.dma_start(cpack[:, :], const_d).then_inc(s_const, 16)

            for c in range(NC_X):
                if c == 2:
                    small_loads()
                n = slice(ENDS[c], ENDS[c + 1])
                sp.dma_start(x_sb[:, n, :], xr[:, n, :]).then_inc(x_in[c], 16)
            sp.dma_start(shw[:, :], shared_w).then_inc(s_shw, 16)
            for m in range(M):
                sp.dma_start(ew[m][:, :], expert_w[m, :, :]).then_inc(w_in[m], 16)

            sp.wait_ge(zdone, 1)
            flat = acc.rearrange("(p r) d -> p (r d)", p=P)
            for k in range(0, flat.shape[1], 1024):
                n = min(1024, flat.shape[1] - k)
                sp.dma_start(flat[:, k:k + n], zeros[:, 0:n]).then_inc(zero_out, 16)
            sp.dma_start(out[T:T + P, :], zeros[:, 0:D]).then_inc(zero_out, 16)
            sp.dma_start(xng[T:T + P, :], zeros[:, 0:ROW]).then_inc(zero_out, 16)

            def step(i, s):
                b = 2 * i + s
                sp.wait_ge(xn_ready, b + 1)
                sp.sem_inc(waited_sp, 1)
                sp.dma_start(xng_x[b, :, :, :], xn[:, s, :, :]).then_inc(xn_out[s], 16)
                sp.wait_ge(cum_ready, b + 1)
                sp.sem_inc(waited_sp, 1)
                sp.dma_start(cum_st[b, :, :, :], cum[:, s, :, :]).then_inc(cum_out[s], 16)
                sp.wait_ge(gw_ready, b + 1)
                sp.sem_inc(waited_sp, 1)
                sp.dma_start(xng_g[b, :, :, :], gw[:, s, :, :]).then_inc(gw_out[s], 16)

            def store_residual(a):
                sp.wait_ge(res_done, a + 1)
                sp.sem_inc(waited_sp, 1)
                sp.dma_start(res_st[a, :, :, :], x_sb[:, bass.ds(TB * a, TB), :]).then_inc(res_out, 16)

            def counts(first, end):
                for s in range(2):
                    sp.wait_ge(cum_out[s], 16 * end // TB // 2)
                for dst, done in (([cumL[:, :, :]] * M, cum_in), ([cumR[:, :, m, :] for m in range(M)], cumR_in)):
                    for m in range(M):
                        src = cum_d.rearrange("(q m) j t -> m j q t", m=M)[m, first:end, :, :]
                        sp.dma_start(dst[m][32 * m + first:32 * m + end, 0:NG, :], src).then_inc(done, 16)

            step(0, 0)
            step(0, 1)
            with sp.Fori(1, B // 2 - 1) as i:
                step(i, 0)
                store_residual(2 * i - 2)
                step(i, 1)
                store_residual(2 * i - 1)
            sp.wait_ge(cumL_zero, 1)
            sp.wait_ge(tab_zero, -(-NGP * M // 8))
            counts(0, NT - 2 * TB)
            step(B // 2 - 1, 0)
            step(B // 2 - 1, 1)
            counts(NT - 2 * TB, NT)
            for a in range(B - 4, B):
                store_residual(a)

            def loads(g):
                for m in range(M):
                    sp.wait_ge(y_ready, UNITS * g + 1 + m)
                    sp.sem_inc(waited_sp, 1)
                    sp.dma_start(ew[m][:, :], expert_w[M * g + M + m, :, :]).then_inc(w_in[m], 16)

            loads(0)
            with sp.Fori(1, NG - 1) as g:
                loads(g)

        @block.gpsimd
        def _(pool):
            pool.memset(half[:, :], -0.5).then_inc(half_done, 1)
            def rstd_of(c):
                n = slice(ENDS[c], ENDS[c + 1])
                pool.wait_ge(half_done, 1)
                pool.wait_ge(var_ready, c + 1)
                pool.tensor_tensor(rstd[:, n], var[:, n], half[:, 0:ENDS[c + 1] - ENDS[c]], ALU.pow).then_inc(rstd_ready, 1)

            wide = [P, TB, D]

            def normalise(b, i, s):
                xb = x_sb[:, bass.ds(TB * b, TB), :]
                tiles = bass.ds(TB * b, TB)
                pool.tensor_tensor(xm[:, :, :], xb, mean[:, tiles].unsqueeze(2).to_broadcast(wide), ALU.subtract).then_inc(xm_ready, 1)
                pool.wait_ge(xm_ready, b + 1)
                pool.wait_ge(xn_out[s], 16 * i)
                pool.wait_ge(xTp_ready, since(b - 1))
                pool.tensor_tensor(xn[:, s, :, :], xm[:, :, :], rstd[:, tiles].unsqueeze(2).to_broadcast(wide), ALU.mult).then_inc(xn_ready, 1)

            def offsets(b, s):
                xb = x_sb[:, bass.ds(TB * b, TB), :]
                tiles = bass.ds(TB * b, TB)
                pool.tensor_tensor(xb, xb, beta_b[:, :].unsqueeze(1).to_broadcast(wide), ALU.add).then_inc(xb_ready, 1)
                pool.wait_ge(xn_ready, b + 1)
                pool.tensor_tensor(xnb[:, tiles, :], xn[:, s, :, :], bo_b[:, :].unsqueeze(1).to_broadcast(wide), ALU.add).then_inc(xb_ready, 1)

            def attention_rstd(a):
                pool.wait_ge(v2_ready, a + 1)
                pool.wait_ge(yn_ready, TB * a)
                pool.tensor_tensor(m2[:, 5, :], m2[:, 4, :], half[:, 0:TB], ALU.pow).then_inc(r2_ready, 1)
                pool.wait_ge(r2_ready, 2 * a + 1)
                pool.tensor_tensor(nb[:, :], m2[:, 3, :], m2[:, 5, :], ALU.mult).then_inc(r2_ready, 1)

            def qk_product(a):
                pool.wait_ge(f_ready, a + 1)
                pool.wait_ge(qks_step, 2 * a)
                pool.tensor_tensor(qk[:, :, :], f[:, :, 0:D], f[:, :, D:2 * D], ALU.mult).then_inc(qk_prod, 1)

            def finish(a):
                xg = x_sb[:, bass.ds(TB * a, TB), :]
                pool.wait_ge(yn_ready, TB * a + TB)
                pool.tensor_tensor(yg[:, :, :], yg[:, :, :], gamma_b[:, :].unsqueeze(1).to_broadcast([P, TB, D]), ALU.mult).then_inc(yg_ready, 1)
                pool.wait_ge(yg_ready, a + 1)
                pool.wait_ge(y_used, a + 1)
                pool.tensor_tensor(xg, xg, yg[:, :, :], ALU.add).then_inc(res_done, 1)

            rstd_of(0)
            pool.wait_ge(rstd_ready, 1)
            pool.wait_ge(s_w, 32)
            normalise(0, 0, 0)
            offsets(0, 0)
            rstd_of(1)
            pool.wait_ge(rstd_ready, 2)
            normalise(1, 0, 1)
            offsets(1, 1)
            rstd_of(2)
            qk_product(0)
            normalise(2, 1, 0)
            offsets(2, 0)
            rstd_of(3)
            rstd_of(4)
            pool.wait_ge(rstd_ready, NC_X)
            def steps(i):
                qk_product(2 * i - 1)
                normalise(2 * i + 1, i, 1)
                attention_rstd(2 * i - 2)
                offsets(2 * i + 1, 1)
                finish(2 * i - 2)
                qk_product(2 * i)
                normalise(2 * i + 2, i + 1, 0)
                attention_rstd(2 * i - 1)
                offsets(2 * i + 2, 0)
                finish(2 * i - 1)

            steps(1)
            with pool.Fori(2, B // 2 - 1) as i:
                steps(i)
            qk_product(B - 3)
            normalise(B - 1, B // 2 - 1, 1)
            attention_rstd(B - 4)
            offsets(B - 1, 1)
            finish(B - 4)
            qk_product(B - 2)
            attention_rstd(B - 3)
            finish(B - 3)
            qk_product(B - 1)
            attention_rstd(B - 2)
            finish(B - 2)
            for s in range(2):
                pool.wait_ge(xn_out[s], 16 * B // 2)
                pool.wait_ge(gw_out[s], 16 * B // 2)
            pool.wait_ge(zero_out, 16 * NZERO)
            added_to = (out, acc)

            def gather(g, p, m):
                if isinstance(g, int) and g == 0:
                    pool.wait_ge(idx_ready, 1)
                else:
                    pool.wait_ge(idx_ready, g + 1)
                    pool.wait_ge(xeP, (M + 1) * (g - 1) + (2 if m in (0, M) else m + 2))
                    pool.sem_inc(waited, 1)
                pool.indirect_dma_start(out=gath[:, p, m, :], out_offset=None, in_=xng,
                                        in_offset=bass.IndirectOffsetOnAxis(ap=idx_g[:, p, m:m + 1], axis=0)
                                        ).then_inc(g_in[m], 16)

            def scatter(g, p, m):
                prev = {0: 3, 1: M, 2: 0, 3: 1, M: 2}[m]
                pool.wait_ge(s_sc[prev], 16 * (g + (1 if m >= 2 else 0)))
                if m < M:
                    pool.wait_ge(idxs_c, g + 1)
                    pool.wait_ge(ys_ready, M * g + m + 1)
                    src = ys[:, m, :]
                else:
                    pool.wait_ge(idxs_ready, g + 1)
                    pool.wait_ge(ysum_ready, g + 1)
                    src = ys[:, M + 1, :]
                pool.sem_inc(waited, 1)
                pool.indirect_dma_start(out=added_to[(p + m) % 2],
                                        out_offset=bass.IndirectOffsetOnAxis(ap=idx_s[:, p, m:m + 1], axis=0),
                                        in_=src, in_offset=None, compute_op=ALU.add).then_inc(s_sc[m], 16)

            def group(g, p, first, last):
                if not first:
                    scatter(g - 1, 1 - p, 2)
                if not last:
                    pool.wait_ge(wrest_done, g)
                    gather(g + 1, 1 - p, M)
                    gather(g + 1, 1 - p, 0)
                if not first:
                    scatter(g - 1, 1 - p, 3)
                if not last:
                    gather(g + 1, 1 - p, 1)
                if not first:
                    scatter(g - 1, 1 - p, M)
                if not last:
                    gather(g + 1, 1 - p, 2)
                scatter(g, p, 0)
                if not last:
                    gather(g + 1, 1 - p, 3)
                scatter(g, p, 1)

            gather(0, 0, M)
            gather(0, 0, 0)
            attention_rstd(B - 1)
            for m in (1, 2, 3):
                gather(0, 0, m)
            finish(B - 1)
            pool.wait_ge(res_out, 16 * B)
            group(0, 0, True, False)
            with pool.Fori(0, NG // 2 - 1) as i:
                group(2 * i + 1, 1, False, False)
                group(2 * i + 2, 0, False, False)
            group(NG - 1, 1, False, True)
            for m in (2, 3, M):
                scatter(NG - 1, 1, m)

            for m in range(M + 1):
                pool.wait_ge(s_sc[m], 16 * NG)
            pool.dma_start(out[0:T, :].rearrange("(p r) d -> p (r d)", p=P), acc[0:T, :].rearrange("(p r) d -> p (r d)", p=P),
                           max_dma_last_dim=4096, accum_op=ALU.add).then_inc(out_sem, 16)
            pool.wait_ge(out_sem, 16)

        @block.scalar
        def _(act):
            act.wait_ge(zdone, 1)
            flat = cumR[:, :, :, :].rearrange("p q m t -> p (q m t)")
            for k in range(0, NGP * M * P, 1024):
                n = min(1024, NGP * M * P - k)
                act.activation(flat[:, k:k + n], zeros[:, 0:n], ACT.Copy).then_inc(tab_zero, 1)
            def shared_silu(a, k):
                act.wait_ge(sh_h2, 2 * a + k + 1)
                act.activation(si[:, k, :, 0:P], sh_view(k, 1), ACT.Silu).then_inc(sh_si, 1)

            def load_exp():
                act.activation(scrap[:, 0:1], half[:, 0:1], ACT.Exp)

            def attention_norm(a, sa):
                act.wait_ge(r2_ready, 2 * a + 2)
                act.wait_ge(res_done, a)
                for j in range(TB):
                    act.activation(yg[:, j, :], y[:, sa, j, :], ACT.Identity, scale=m2[:, 5, j:j + 1], bias=nb[:, j:j + 1]).then_inc(yn_ready, 1)

            def rows_copy(b, s):
                act.wait_ge(xTp_ready, b + 1)
                act.activation(xT[:, s, :], RT[:, 0:L], ACT.Copy).then_inc(xT_ready, 1)

            def step(b, s, attend, finish, more):
                a = None if not attend else b - 1 if b is not None else B - 1
                if attend:
                    act.wait_ge(u_ready, a + 1)
                    act.wait_ge(f_ready, a)
                    act.activation(eu[:, :, :], u1[:, :, :], ACT.Exp, bias=cols[:, 7:8]).then_inc(eu_ready, 1)
                    act.wait_ge(v_ready, a + 1)
                    act.wait_ge(o_ready, a)
                    act.activation(vT[:, :], AV[1 - s][:, 0:L], ACT.Identity, bias=bvc[:, 0:1]).then_inc(vT_done, 1)
                if b is not None:
                    act.wait_ge(nmax_ready, b + 1)
                    act.wait_ge(gw_ready, since(b - 1))
                    for j in range(TB):
                        act.activation(ex[:, s, j, :], LG[:, j * E:(j + 1) * E], ACT.Exp,
                                       bias=nmax[:, s, j:j + 1], accum_out=esum[:, s, j:j + 1]).then_inc(ex_ready, 1)
                if attend:
                    shared_silu(a, 0)
                    shared_silu(a, 1)
                if b is not None:
                    act.wait_ge(cump_ready, b + 1)
                    act.wait_ge(cum_out[s], 16 * ((b - s) // 2 if isinstance(b, int) else ring_i))
                    act.activation(cum[:, s, :, :], RT[0:E, 0:L].rearrange("e (j t) -> e j t", j=TB),
                                   ACT.Copy).then_inc(cum_ready, 1)
                if attend:
                    act.wait_ge(oTp_ready, a + 1)
                    act.wait_ge(z_ready, a)
                    act.activation(oT_s[:, :], AV[1 - s][:, 0:L], ACT.Copy).then_inc(oT_done, 1)
                if more:
                    rows_copy(b + 1, 1 - s)
                if finish:
                    attention_norm(a - 1, s)
                if b is not None:
                    load_exp()

            act.wait_ge(half_done, 1)
            rows_copy(0, 0)
            step(0, 0, False, False, True)
            step(1, 1, True, False, True)
            step(2, 0, True, True, True)
            step(3, 1, True, True, True)
            with act.Fori(2, B // 2 - 1) as ring_i:
                step(2 * ring_i, 0, True, True, True)
                step(2 * ring_i + 1, 1, True, True, True)
            step(B - 2, 0, True, True, True)
            step(B - 1, 1, True, True, False)
            step(None, 0, True, True, False)

            def silu(g, u):
                act.wait_ge(h2_ready, UNITS * g + u + 1)
                act.activation(si[:, u % 2, :, :], hview(u, 1, CAP), ACT.Silu).then_inc(si_ready, 1)

            def xe_copy(g, p, k):
                if k == 0:
                    act.wait_ge(xeP, (M + 1) * g + 2)
                    act.activation(xe[:, p, :, P:CAP], X[:, 0:P].rearrange("p (m r) -> p m r", m=M),
                                   ACT.Copy).then_inc(xe_done, 1)
                else:
                    act.wait_ge(xeP, (M + 1) * g + k + 1)
                    r = 1 if k == 1 else 0
                    act.activation(xe[:, p, k - 1, 0:P], X[:, r * P:(r + 1) * P], ACT.Copy).then_inc(xe_done, 1)

            def y_copy(g, p, m):
                act.wait_ge(y_ready, UNITS * g + 1 + m)
                act.wait_ge(s_sc[m], 16 * g)
                act.activation(ys[:, m, :], Y[m % 2][:, 0:P], ACT.Copy,
                               scale=gath[:, p, m, bass.ds(D + M * g + m, 1)]).then_inc(ys_ready, 1)

            def narrow_copy(q):
                act.wait_ge(tab_mm, q + 1)
                act.wait_ge(idx_ready, q)
                act.activation(nar[:, :], X[:, 0:P + 2 * (M + 1)], ACT.Copy).then_inc(nar_done, 1)

            def rest_copy(g, p):
                act.wait_ge(wrest_done, g + 1)
                act.wait_ge(y_ready, UNITS * (g + 1))
                act.activation(ys[:, M, :], R[:, 0:P], ACT.Copy, scale=wrest[:, p:p + 1]).then_inc(rest_done, 1)

            def sum_copy(g):
                act.wait_ge(sum_mm, g + 1)
                act.wait_ge(s_sc[M], 16 * g)
                act.activation(ys[:, M + 1, :], A[:, 0:P], ACT.Copy).then_inc(ysum_ready, 1)

            def group(g, p, first, last):
                if not first:
                    y_copy(g - 1, 1 - p, 2)
                silu(g, 0)
                xe_copy(g, p, 2)
                if not first:
                    y_copy(g - 1, 1 - p, 3)
                    rest_copy(g - 1, 1 - p)
                silu(g, 1)
                xe_copy(g, p, 3)
                if not first:
                    sum_copy(g - 1)
                y_copy(g, p, 0)
                silu(g, 2)
                xe_copy(g, p, 4)
                y_copy(g, p, 1)
                if not last:
                    narrow_copy(g + 2)
                silu(g, 3)
                if not last:
                    xe_copy(g + 1, 1 - p, 0)
                    xe_copy(g + 1, 1 - p, 1)

            narrow_copy(0)
            narrow_copy(1)
            xe_copy(0, 0, 0)
            xe_copy(0, 0, 1)
            attention_norm(B - 1, 1)
            group(0, 0, True, False)
            with act.Fori(0, NG // 2 - 1) as i:
                group(2 * i + 1, 1, False, False)
                group(2 * i + 2, 0, False, False)
            group(NG - 1, 1, False, True)
            y_copy(NG - 1, 1, 2)
            y_copy(NG - 1, 1, 3)
            rest_copy(NG - 1, 1)
            sum_copy(NG - 1)

        @block.vector
        def _(dve):
            dve.memset(ones[:, :], 1.0).then_inc(set_done, 1)
            dve.memset(zeros[:, :], 0.0).then_inc(zdone, 1)
            dve.memset(cumL[:, :, :], 0.0).then_inc(cumL_zero, 1)
            def fold():
                dve.wait_ge(s_const, 16)
                dve.tensor_copy(upper[:, :], upper_f[:, :]).then_inc(cast_done, 1)
                dve.tensor_copy(before[:, :], before_f[:, :]).then_inc(cast_done, 1)
                dve.tensor_copy(slot[:, :], slot_f[:, :]).then_inc(cast_done, 1)
                dve.wait_ge(s_w, 32)
                dve.wait_ge(set_done, 1)
                for k in range(2):
                    dve.tensor_scalar(brep[:, k, :], ones[:, :], bcol[:, k:k + 1], None, ALU.mult).then_inc(cast_done, 1)
                dve.wait_ge(fold_mm, 1)
                dve.tensor_copy(wqk[:, :], bank[4][:, 0:2 * D]).then_inc(fold_done, 1)
                dve.tensor_copy(wv[:, :], bank[4][:, 2 * D:3 * D]).then_inc(fold_done, 1)
                dve.scalar_tensor_tensor(bqk1[:, :], bank[7][:, 0:2 * D], 1.0, brow[:, :, :].rearrange("p a n -> p (a n)"),
                                         ALU.add, ALU.add).then_inc(fold_done, 1)
                dve.tensor_tensor(bvc[:, :], bank[7][:, 2 * D:2 * D + 1], bcol[:, 3:4], ALU.add).then_inc(fold_done, 1)

            def statistics(c):
                n = slice(ENDS[c], ENDS[c + 1])
                dve.wait_ge(x_in[c], 16)
                for t in range(ENDS[c], ENDS[c + 1]):
                    dve.bn_stats(st[:, t, :], x_sb[:, t, :]).then_inc(stat_d, 1)
                k = ENDS[c + 1] + 6 * c
                moments(dve, st[:, n, :], m_t[:, :, 0:ENDS[c + 1] - ENDS[c]], mean[:, n], var[:, n], stat_d, k, EPS_LN, var_ready)

            statistics(0)
            statistics(1)
            fold()
            def shared_act(a, k):
                dve.wait_ge(sh_si, 2 * a + k + 1)
                dve.wait_ge(sh_h, 2 * a + k + 1)
                dve.wait_ge(sh_y, 2 * a)
                dve.tensor_tensor(ac[:, k, :, 0:P], si[:, k, :, 0:P], sh_view(k, 0), ALU.mult).then_inc(sh_ac, 1)

            def attention_y(a, sa):
                dve.wait_ge(z_ready, a + 1)
                dve.wait_ge(xb_ready, 2 * a + 2)
                dve.tensor_tensor(y[:, sa, :, :], AQ[sa][:, 0:TB * D].rearrange("p (j n) -> p j n", j=TB),
                                  xnb[:, bass.ds(TB * a, TB), :], ALU.add).then_inc(z_used, 1)

            def shared_add(a):
                tiles = bass.ds(TB * a, TB)
                dve.wait_ge(sh_y, 2 * a + 2)
                dve.tensor_tensor(x_sb[:, tiles, :], x_sb[:, tiles, :], YS[:, 0:TB * D].rearrange("p (j n) -> p j n", j=TB), ALU.add).then_inc(y_used, 1)

            def attention_stats(a, sa):
                dve.wait_ge(z_used, a + 1)
                for j in range(TB):
                    dve.bn_stats(st2[:, j, :], y[:, sa, j, :]).then_inc(y_step, 1)

            def attention_moments(a, stage):
                if stage == 1:
                    dve.wait_ge(r2_ready, 2 * a)
                    dve.wait_ge(yn_ready, TB * a)
                moments(dve, st2[:, :, :], m2, m2[:, 3, :], m2[:, 4, :], y_step, 8 * a + 2, EPS_ATT, v2_ready, sign=-1.0, stages=(stage,))

            def tiles_before():
                dve.wait_ge(cum_in, 2 * 16 * M)
                dve.tensor_copy(cnt_f[:, :], cumL[:, :, P - 1]).then_inc(cntf_done, 1)
                dve.wait_ge(base_mm, 1)
                dve.tensor_copy(base[:, :], bank[5][:, 0:NGP]).then_inc(base_done, 1)
                dve.wait_ge(cntf_done, 1)
                dve.tensor_tensor(nxt[:, :], bank[5][:, 0:NGP], cnt_f[:, :], ALU.add).then_inc(base_done, 1)
                dve.wait_ge(base_done, 2)
                for m in range(M):
                    dve.tensor_scalar(jb[:, :, m, 1], base[:, :], block4[:, m:m + 1], None, ALU.mult).then_inc(jb_done, 1)
                dve.tensor_copy(jb[:, :, M, 1], base[:, :]).then_inc(jb_done, 1)
                dve.tensor_copy(jb[:, :, :, 0], jrow[:, :].unsqueeze(1).to_broadcast([P, NGP, M + 1])).then_inc(jb_done, 1)

            def table_hot(q):
                dve.wait_ge(tab_mm, q)
                dve.tensor_scalar(ge[:, :], slot[:, :], base[:, bass.ds(q, 1)], None, ALU.is_ge).then_inc(oh_ready, 1)
                dve.wait_ge(oh_ready, 3 * q + 1)
                dve.scalar_tensor_tensor(oh[:, :], slot[:, :], nxt[:, bass.ds(q, 1)], ge[:, :], ALU.is_lt, ALU.mult).then_inc(oh_ready, 1)
                dve.wait_ge(oh_ready, 3 * q + 2)
                dve.tensor_tensor(ohr[:, :, :], oh[:, P:CAP].unsqueeze(1).to_broadcast([P, M, REST]),
                                  block4[:, :].unsqueeze(2).to_broadcast([P, M, REST]), ALU.mult).then_inc(oh_ready, 1)

            def step(b, s, attend, finish):
                route = b is not None
                a = None if not attend else b - 1 if route else B - 1
                if finish:
                    attention_y(a - 1, s)
                if attend:
                    dve.wait_ge(qk_ready, a + 1)
                    dve.wait_ge(eu_ready, a)
                    dve.tensor_tensor(u1[:, :, :], AQ[1 - s][:, :].rearrange("p (j n) -> p j n", j=TB),
                                      bqk1[:, :].unsqueeze(1).to_broadcast([P, TB, 2 * D]), ALU.add).then_inc(u_ready, 1)
                if route:
                    dve.wait_ge(logit_ready, b + 1)
                    dve.wait_ge(ex_ready, since(2 * b - 2))
                    dve.tensor_reduce(nmax[:, s, :], LG[:, 0:TB * E].rearrange("p (j e) -> p j e", j=TB),
                                      AX.X, ALU.max, negate=True).then_inc(nmax_ready, 1)
                if finish:
                    attention_stats(a - 1, s)
                if attend:
                    dve.wait_ge(eu_ready, a + 1)
                    dve.wait_ge(S_ready, a)
                    dve.wait_ge(qk_prod, a)
                    dve.scalar_tensor_tensor(f[:, :, :].rearrange("p j n -> p (j n)"), eu[:, :, :].rearrange("p j n -> p (j n)"), 1.0,
                                             u1[:, :, :].rearrange("p j n -> p (j n)"), ALU.min, ALU.max).then_inc(f_ready, 1)
                if finish:
                    attention_moments(a - 1, 0)
                    shared_add(a - 1)
                if route:
                    dve.wait_ge(ex_ready, 2 * b + 2)
                    dve.reciprocal(rs[:, s, :], esum[:, s, :]).then_inc(gate_c, 1)
                    for j in range(TB):
                        dve.max(top[:, s, j, :], ex[:, s, j, :]).then_inc(top_ready, 1)
                if finish:
                    attention_moments(a - 1, 1)
                if attend:
                    dve.wait_ge(S_ready, a + 1)
                    dve.wait_ge(o_ready, a)
                    dve.tensor_tensor(S_s[:, :], AV[1 - s][:, 0:P], head[:, :], ALU.mult).then_inc(Ss_done, 1)
                    dve.wait_ge(qk_prod, a + 1)
                    dve.tensor_reduce(qks[:, :, :], qk[:, :, :].rearrange("p j (h d) -> p j h d", h=H), AX.X, ALU.add).then_inc(qks_step, 1)
                if finish:
                    attention_moments(a - 1, 2)
                if route:
                    dve.wait_ge(top_ready, 2 * b + 2)
                    dve.tensor_reduce(tsum[:, s, :], top[:, s, :, :], AX.X, ALU.add).then_inc(gate_c, 1)
                if attend:
                    dve.wait_ge(qks_step, 2 * a + 1)
                    dve.tensor_scalar(qks[:, :, :], qks[:, :, :], EPS_QK, None, ALU.add).then_inc(qks_step, 1)
                if route:
                    for j in range(TB):
                        dve.match_replace(left[:, s, j, :], top[:, s, j, :], ex[:, s, j, :], -1.0).then_inc(left_ready, 1)
                if attend:
                    dve.wait_ge(qks_step, 2 * a + 2)
                    dve.reciprocal(rq[:, :, :], qks[:, :, :]).then_inc(rq_ready, 1)
                if finish:
                    attention_moments(a - 1, 3)
                if route:
                    dve.wait_ge(left_ready, 2 * b + 2)
                    dve.wait_ge(cump_ready, since(b - 1))
                    dve.tensor_scalar(mask[:, s, :, :], left[:, s, :, :], 0.0, None, ALU.is_lt).then_inc(mask_ready, 1)
                    dve.wait_ge(gate_c, 4 * b + 2)
                    dve.tensor_tensor(den[:, s, :], tsum[:, s, :], rs[:, s, :], ALU.mult).then_inc(gate_c, 1)
                if attend:
                    dve.wait_ge(o_ready, a + 1)
                    dve.wait_ge(rq_ready, a + 1)
                    dve.wait_ge(oTp_ready, a)
                    dve.tensor_tensor(o_s[:, :, :].rearrange("p j (h d) -> p (j h) d", h=H),
                                      AQ[1 - s][:, 0:TB * D].rearrange("p (n d) -> p n d", d=DH),
                                      rq[:, :, :].rearrange("p j h -> p (j h)").unsqueeze(2).to_broadcast([P, TB * H, DH]),
                                      ALU.mult).then_inc(o_done, 1)
                    shared_act(a, 0)
                if route:
                    dve.wait_ge(gate_c, 4 * b + 3)
                    dve.tensor_scalar(den[:, s, :], den[:, s, :], F32_EPS, None, ALU.max).then_inc(gate_c, 1)
                if route:
                    dve.wait_ge(gate_c, 4 * b + 4)
                    dve.reciprocal(wt[:, s, :], den[:, s, :]).then_inc(wt_c, 1)
                if attend and not route:
                    tiles_before()
                    table_hot(0)
                if attend:
                    shared_act(a, 1)
                if route:
                    dve.wait_ge(wt_c, 2 * b + 1)
                    dve.tensor_tensor(wt[:, s, :], wt[:, s, :], rs[:, s, :], ALU.mult).then_inc(wt_c, 1)
                    dve.wait_ge(wt_c, 2 * b + 2)
                    dve.wait_ge(gw_out[s], 16 * ((b - s) // 2 if isinstance(b, int) else ring_i))
                    dve.tensor_tensor(gw[:, s, :, :], ex[:, s, :, :], wt[:, s, :].unsqueeze(2).to_broadcast([P, TB, E]),
                                      ALU.mult).then_inc(gw_ready, 1)

            step(0, 0, False, False)
            statistics(2)
            step(1, 1, True, False)
            statistics(3)
            statistics(4)
            step(2, 0, True, True)
            step(3, 1, True, True)
            with dve.Fori(2, B // 2) as ring_i:
                step(2 * ring_i, 0, True, True)
                step(2 * ring_i + 1, 1, True, True)
            step(None, 0, True, True)
            attention_y(B - 1, 1)

            small = nar[:, P:P + 2 * (M + 1)].rearrange("p (k a) -> p k a", a=2)
            N = 8

            def table_compare(q):
                dve.wait_ge(nar_done, q + 1)
                dve.tensor_tensor(thr[:, :], cols[:, 0:M + 1], small[:, :, 1], ALU.subtract).then_inc(tab_step, 1)
                dve.wait_ge(tab_step, N * q + 1)
                dve.tensor_tensor(le[:, 0:M, :], A[:, :].rearrange("p (m t) -> p m t", m=M),
                                  thr[:, 0:M].unsqueeze(2).to_broadcast([P, M, P]), ALU.is_le).then_inc(tab_step, 1)
                dve.tensor_scalar(le[:, M, :], nar[:, 0:P], thr[:, M:M + 1], None, ALU.is_le).then_inc(tab_step, 1)
                dve.tensor_scalar(hit[:, :], small[:, :, 0], 0.0, None, ALU.is_gt).then_inc(tab_step, 1)

            def table_tokens(q, p):
                dve.wait_ge(tab_step, N * q + 4)
                dve.tensor_reduce(cnt[:, :], le[:, :, :], AX.X, ALU.add).then_inc(tab_step, 1)
                dve.wait_ge(tab_step, N * q + 5)
                dve.scalar_tensor_tensor(tok[:, :], small[:, :, 0], float(P), cnt[:, :], ALU.mult, ALU.add).then_inc(tab_step, 1)
                dve.wait_ge(tab_step, N * q + 6)
                dve.scalar_tensor_tensor(tok[:, :], tok[:, :], cols[:, 6:7], hit[:, :], ALU.subtract, ALU.mult).then_inc(tab_step, 1)
                dve.wait_ge(tab_step, N * q + 7)
                dve.tensor_scalar(v_all[:, q, :], tok[:, :], cols[:, 5:6], None, ALU.add).then_inc(tab_step, 1)
                dve.tensor_scalar(idx_g[:, p, :], tok[:, :], cols[:, 5:6], None, ALU.add).then_inc(idx_ready, 1)

            def act_mul(g, u):
                dve.wait_ge(si_ready, UNITS * g + u + 1)
                dve.wait_ge(h_ready, UNITS * g + u + 1)
                dve.wait_ge(y_ready, since(UNITS * g + u - 1))
                dve.tensor_tensor(ac[:, u % 2, :, :], si[:, u % 2, :, :], hview(u, 0, CAP), ALU.mult).then_inc(ac_ready, 1)

            def group(g, p, first, last):
                vM = v_all[:, g, M:M + 1]
                dve.wait_ge(idx_ready, g + 1)
                if not first:
                    act_mul(g - 1, 3)
                if not last:
                    table_tokens(g + 1, 1 - p)
                dve.wait_ge(vrepT_ready, g)
                dve.tensor_scalar(vrep[:, :], ones[:, :], vM, None, ALU.mult).then_inc(vrep_ready, 1)
                dve.wait_ge(vrepT_ready, g + 1)
                dve.wait_ge(sum_mm, since(g - 1))
                dve.tensor_scalar(eq[:, p, :], A[:, 0:P], vM, None, ALU.is_equal).then_inc(eq_step, 1)
                act_mul(g, 0)
                if not first:
                    dve.wait_ge(s_sc[3], 16 * (g - 1))
                    dve.wait_ge(s_sc[M], 16 * (g - 1))
                dve.tensor_copy(idx_s[:, p, 0:M], idx_g[:, p, 0:M]).then_inc(idxs_c, 1)
                dve.tensor_tensor(wr_t[:, :], gath[:, p, M, bass.ds(D + M * g, M)], block4[:, :], ALU.mult).then_inc(wrest_c, 1)
                dve.wait_ge(wrest_c, g + 1)
                dve.wait_ge(rest_done, since(g - 1))
                dve.tensor_reduce(wrest[:, p:p + 1], wr_t[:, :], AX.X, ALU.add).then_inc(wrest_done, 1)
                if not last:
                    table_hot(g + 2)
                act_mul(g, 1)
                dve.wait_ge(eq_step, 5 * g + 1)
                dve.tensor_tensor(dup_t[:, :], eq[:, p, :], earlier[:, :], ALU.mult).then_inc(eq_step, 1)
                dve.wait_ge(eq_step, 5 * g + 2)
                dve.tensor_reduce(dup[:, :], dup_t[:, :], AX.X, ALU.add).then_inc(eq_step, 1)
                dve.wait_ge(eq_step, 5 * g + 3)
                dve.tensor_scalar(first_[:, :], dup[:, :], 0.5, None, ALU.is_lt).then_inc(eq_step, 1)
                dve.wait_ge(eq_step, 5 * g + 4)
                dve.scalar_tensor_tensor(vr[:, :], vM, cols[:, 5:6], first_[:, :], ALU.subtract, ALU.mult).then_inc(eq_step, 1)
                dve.wait_ge(eq_step, 5 * g + 5)
                dve.tensor_scalar(idx_s[:, p, M:M + 1], vr[:, :], cols[:, 5:6], None, ALU.add).then_inc(idxs_ready, 1)
                act_mul(g, 2)
                if not last:
                    table_compare(g + 2)

            dve.wait_ge(jb_done, M + 2)
            table_compare(0)
            table_tokens(0, 0)
            shared_add(B - 1)
            attention_stats(B - 1, 1)
            for stage in range(4):
                attention_moments(B - 1, stage)
            table_hot(1)
            table_compare(1)
            group(0, 0, True, False)
            with dve.Fori(0, NG // 2 - 1) as i:
                group(2 * i + 1, 1, False, False)
                group(2 * i + 2, 0, False, False)
            group(NG - 1, 1, False, True)
            act_mul(NG - 1, 3)

        @block.tensor
        def _(pe):
            pe.wait_ge(s_w, 32)
            pe.matmul(bank[4][:, 0:D], wqT_s[:, :], w2_s[:, 0, :], start=True, stop=True)
            pe.matmul(bank[4][:, D:2 * D], wkT_s[:, :], w2_s[:, 1, :], start=True, stop=True)
            pe.matmul(bank[4][:, 2 * D:3 * D], wvT_s[:, :], w2_s[:, 2, :], start=True, stop=True)
            pe.wait_ge(cast_done, 5)
            for k in range(2):
                pe.matmul(bank[7][:, k * D:(k + 1) * D], brep[:, k, :], w2_s[:, k, :], start=True, stop=True)
            pe.matmul(bank[7][:, 2 * D:2 * D + 1], w2_s[:, 2, :], bcol[:, 2:3], start=True, stop=True).then_inc(fold_mm, 1)
            def tiles_before():
                pe.wait_ge(cum_in, 2 * 16 * M)
                pe.wait_ge(cum_ready, B)
                pe.matmul(RT[:, 0:NGP], before[:, :], cumL[:, :, P - 1], start=True, stop=True).then_inc(base_mm, 1)

            def table(q):
                pe.wait_ge(oh_ready, 3 * q + 3)
                pe.matmul(A[:, :], oh[:, 0:P], cumR[:, q, :, :].rearrange("p m t -> p (m t)"), start=True, stop=True)
                pe.matmul(X[:, P:P + 8], oh[:, 0:P], jb[:, q, 0:M, :].rearrange("p m a -> p (m a)"), start=True, stop=True)
                pe.matmul(X[:, 0:P], ohr[:, :, :].rearrange("p m r -> p (m r)"), cumL[:, q, :], start=True, stop=True)
                pe.matmul(X[:, P + 8:P + 10], ohr[:, :, :].rearrange("p m r -> p (m r)"), jb[:, q, M, :], start=True, stop=True).then_inc(tab_mm, 1)

            def shared_h(a, k, sa, half_):
                pe.wait_ge(sh_ac, 2 * a)
                if (k, half_) == (1, 0):
                    pe.wait_ge(ex_ready, 2 * min(a + 2, B) if isinstance(a, int) else 2 * a + 4)
                for c in range(FC):
                    w = shw[:, (half_ * FC + c) * P:(half_ * FC + c + 1) * P]
                    last = pe.matmul(sh_view(k, half_)[:, c, :], w, xT[:, sa, k * P:(k + 1) * P], start=True, stop=True)
                last.then_inc(sh_h2 if half_ else sh_h, 1)

            def shared_down(a, k):
                pe.wait_ge(sh_ac, 2 * a + k + 1)
                pe.wait_ge(y_used, a)
                for c in range(FC):
                    last = pe.matmul(YS[:, k * P:(k + 1) * P], ac[:, k, c, 0:P], shw[:, (2 * FC + c) * P:(2 * FC + c + 1) * P],
                                     start=(c == 0), stop=(c == FC - 1))
                last.then_inc(sh_y, 1)

            def rows_up(b, s):
                pe.wait_ge(xn_ready, b + 1)
                pe.wait_ge(cum_ready, b)
                for j in range(TB):
                    last = pe.transpose(RT[:, j * P:(j + 1) * P], xn[:, s, j, :], ident[:, :])
                last.then_inc(xTp_ready, 1)

            def logits(b, s):
                pe.wait_ge(xT_ready, b + 1)
                pe.wait_ge(sh_ac, since(2 * b - 2))
                pe.wait_ge(ex_ready, 2 * b)
                for j in range(TB):
                    last = pe.matmul(LG[:, j * E:(j + 1) * E], xT[:, s, j * P:(j + 1) * P], wg_s[:, :], start=True, stop=True)
                last.then_inc(logit_ready, 1)

            def counts(b, s):
                pe.wait_ge(mask_ready, b + 1)
                for j in range(TB):
                    last = pe.matmul(RT[0:E, j * P:(j + 1) * P], mask[:, s, j, :], upper[:, :], start=True, stop=True)
                last.then_inc(cump_ready, 1)

            def queries_keys(a, sa):
                pe.wait_ge(oT_done, a)
                for j in range(TB):
                    last = pe.matmul(AQ[sa][:, j * 2 * D:(j + 1) * 2 * D], xT[:, sa, j * P:(j + 1) * P], wqk[:, :], start=True, stop=True)
                last.then_inc(qk_ready, 1)

            def values(a, sa):
                pe.wait_ge(z_used, a)
                pe.matmul(AV[sa][:, 0:L], wv[:, :], xT[:, sa, :], start=True, stop=True).then_inc(v_ready, 1)

            def keys_queries(a, sa):
                pe.wait_ge(f_ready, a + 1)
                pe.wait_ge(vT_done, a + 1)
                for j in range(TB):
                    last = pe.matmul(AV[sa][:, 0:P], f[:, j, D:2 * D], f[:, j, 0:D], start=(j == 0), stop=(j == TB - 1))
                last.then_inc(S_ready, 1)

            def attention_out(a, sa):
                pe.wait_ge(Ss_done, a + 1)
                for j in range(TB):
                    last = pe.matmul(AQ[sa][:, j * D:(j + 1) * D], vT[:, j * P:(j + 1) * P], S_s[:, :], start=True, stop=True)
                last.then_inc(o_ready, 1)

            def out_T(a, sa):
                pe.wait_ge(o_done, a + 1)
                for j in range(TB):
                    last = pe.transpose(AV[sa][:, j * P:(j + 1) * P], o_s[:, j, :], ident[:, :])
                last.then_inc(oTp_ready, 1)

            def out_projection(a, sa):
                pe.wait_ge(oT_done, a + 1)
                for j in range(TB):
                    last = pe.matmul(AQ[sa][:, j * D:(j + 1) * D], oT_s[:, j * P:(j + 1) * P], wo_s[:, :], start=True, stop=True)
                last.then_inc(z_ready, 1)

            def step(b, s, attend, more):
                route = b is not None
                a = None if not attend else b - 1 if route else B - 1
                sa = 1 - s
                if attend:
                    shared_h(a, 0, sa, 1)
                    keys_queries(a, sa)
                    shared_h(a, 1, sa, 1)
                    attention_out(a, sa)
                    shared_h(a, 0, sa, 0)
                    shared_h(a, 1, sa, 0)
                if not route:
                    tiles_before()
                if route:
                    counts(b, s)
                if attend:
                    out_T(a, sa)
                if more:
                    rows_up(b + 1, sa)
                if attend:
                    out_projection(a, sa)
                if route:
                    queries_keys(b, s)
                if more:
                    logits(b + 1, sa)
                if route:
                    values(b, s)
                if attend:
                    shared_down(a, 0)
                    shared_down(a, 1)

            rows_up(0, 0)
            logits(0, 0)
            pe.wait_ge(fold_done, 4)
            pe.wait_ge(s_shw, 16)
            step(0, 0, False, True)
            step(1, 1, True, True)
            with pe.Fori(1, B // 2 - 1) as i:
                step(2 * i, 0, True, True)
                step(2 * i + 1, 1, True, True)
            step(B - 2, 0, True, True)
            step(B - 1, 1, True, False)
            step(None, 0, True, False)
            def up(g, p, u):
                pe.wait_ge(xe_done, (M + 1) * g + u + 2)
                pe.wait_ge(w_in[u], 16 * g + 16)
                for half_ in (1, 0):
                    if u > 0 and half_ == 1:
                        pe.wait_ge(ac_ready, since(UNITS * g + u - 1))
                    else:
                        pe.wait_ge(si_ready, UNITS * g + u)
                        if u == 0 and half_ == 0:
                            pe.wait_ge(ac_ready, UNITS * g)
                    for c in range(FC):
                        k = half_ * FC + c
                        last = pe.matmul(hview(u, half_, CAP)[:, c, :], ew[u][:, k * P:(k + 1) * P], xe[:, p, u, :], start=True, stop=True)
                    last.then_inc(h2_ready if half_ else h_ready, 1)

            def down(g, m):
                r = m % 2
                pe.wait_ge(ac_ready, UNITS * g + m + 1)
                pe.wait_ge(ys_ready, since(M * g + m - 1))
                for c in range(FC):
                    pe.matmul(Y[r][:, 0:P], ac[:, r, c, 0:P], ew[m][:, (6 + c) * P:(7 + c) * P],
                              start=(c == 0), stop=(c == FC - 1))
                if m == 0:
                    pe.wait_ge(rest_done, g)
                for c in range(FC):
                    last = pe.matmul(R[32 * m:32 * m + 32, 0:P], ac[:, r, c, P:CAP], ew[m][:, (6 + c) * P:(7 + c) * P],
                                     start=(c == 0), stop=(c == FC - 1))
                last.then_inc(y_ready, 1)

            def rows_T(g, p, k):
                if k == 1:
                    pe.wait_ge(nar_done, g + 2)
                    pe.wait_ge(g_in[M], 16 * g + 16)
                    pe.transpose(X[:, 0:P], gath[:, p, M, 0:D], ident[:, :])
                    pe.wait_ge(g_in[0], 16 * g + 16)
                    pe.transpose(X[:, P:2 * P], gath[:, p, 0, 0:D], ident[:, :]).then_inc(xeP, 2)
                else:
                    pe.wait_ge(g_in[k - 1], 16 * g + 16)
                    pe.wait_ge(xe_done, (M + 1) * g + k)
                    pe.transpose(X[:, 0:P], gath[:, p, k - 1, 0:D], ident[:, :]).then_inc(xeP, 1)

            def rest_sum(g, p):
                pe.wait_ge(rest_done, g + 1)
                pe.matmul(A[:, 0:P], eq[:, p, :], ys[:, M, :], start=True, stop=True).then_inc(sum_mm, 1)

            def group(g, p, first, last):
                up(g, p, 0)
                rows_T(g, p, 2)
                if not first:
                    down(g - 1, 3)
                pe.wait_ge(vrep_ready, g + 1)
                pe.wait_ge(tab_step, 8 * (g + 1) + 2)
                pe.transpose(A[:, 0:P], vrep[:, :], ident[:, :]).then_inc(vrepT_ready, 1)
                up(g, p, 1)
                rows_T(g, p, 3)
                pe.wait_ge(eq_step, 5 * g + 1)
                if not first:
                    rest_sum(g - 1, 1 - p)
                down(g, 0)
                up(g, p, 2)
                rows_T(g, p, 4)
                down(g, 1)
                if not last:
                    pe.wait_ge(ysum_ready, g)
                    pe.wait_ge(xe_done, (M + 1) * (g + 1))
                    table(g + 2)
                up(g, p, 3)
                if not last:
                    rows_T(g + 1, 1 - p, 1)
                down(g, 2)

            pe.wait_ge(jb_done, M + 2)
            pe.wait_ge(cumR_in, 2 * 16 * M)
            pe.wait_ge(oT_done, B)
            pe.wait_ge(sh_ac, 2 * B)
            table(0)
            pe.wait_ge(idx_ready, 1)
            table(1)
            rows_T(0, 0, 1)
            group(0, 0, True, False)
            with pe.Fori(0, NG // 2 - 1) as i:
                group(2 * i + 1, 1, False, False)
                group(2 * i + 2, 0, False, False)
            group(NG - 1, 1, False, True)
            down(NG - 1, 3)
            rest_sum(NG - 1, 1)


def kernel(**inputs):
    import numpy as _np
    import concourse.bacc as _bacc
    from concourse import mybir as _mybir
    from concourse.bass_utils import run_bass_kernel_spmd as _run

    a = {n: _np.asarray(v) for n, v in inputs.items()}
    P, M = 128, 4
    x = a['L0_attn_x']
    B, L, D = x.shape
    NT = B * L // P

    def packed(w1, w2):
        up = _np.swapaxes(w1, -1, -2)
        down = _np.swapaxes(w2, -1, -2)
        c = down.shape[-2] // P
        down = down.reshape(down.shape[:-2] + (c, P, D))
        down = _np.swapaxes(down, -3, -2).reshape(down.shape[:-3] + (P, c * D))
        return _np.concatenate([up, down], axis=-1)

    def layer(n):
        return a['L0_attn_' + n]

    arrays = {'x': x}
    arrays['weights'] = _np.concatenate(
        [layer('Wq').T, layer('Wk').T, layer('Wv').T, layer('Wq2'), layer('Wk2'), layer('Wv2'), layer('Wo'),
         a['L0_ffn_wg'].T] + [layer(n)[:, None] for n in ('bq', 'bk', 'bv', 'bv2')], axis=1)
    arrays['vectors'] = _np.concatenate([layer(n) for n in ('bq2', 'bk2', 'bo', 'gamma', 'beta')])
    arrays['shared_w'] = packed(a['L0_ffn_shared_w1'], a['L0_ffn_shared_w2'])
    arrays['expert_w'] = packed(a['L0_ffn_expert_w1'], a['L0_ffn_expert_w2'])

    p = _np.arange(P)
    row, col = p[:, None], p[None, :]
    rest = P + p % 32
    cols = _np.stack([p, p, p, p, rest, B * L + p, B * L + p + P, -_np.ones(P)], axis=1)
    block4 = (row // 32 == _np.arange(M)[None, :])
    jrow = _np.concatenate([block4 * (row % 32 + 1), row % 32 + 1], axis=1)
    constants = [
        row == col,
        row <= col,
        (row // 32 == col // 32) & (row < col),
        col < row,
        row // 8 == col // 8,
        _np.broadcast_to(_np.arange(160)[None, :], (P, 160)),
        cols, block4, jrow]
    arrays['constants'] = _np.concatenate(constants, axis=1).astype(_np.float32)

    nc = _bacc.Bacc("TRN2", target_bir_lowering=False, num_devices=1)
    given, args = {}, []
    for n, v in arrays.items():
        v = _np.ascontiguousarray(v)
        given[f"in_{n}"] = v
        args.append(nc.dram_tensor(f"in_{n}", v.shape, _mybir.dt.from_np(v.dtype), kind="ExternalInput").ap())
    args.append(nc.dram_tensor("out_0", (B * L + P, D), _mybir.dt.float32, kind="ExternalOutput").ap())
    block_kernel(nc, *args)
    r = _run(nc, [given], core_ids=[0])
    return r.results[0]["out_0"][:B * L].reshape(B, L, D)
```
